# Optimizing a Trainium2 kernel written in Bass

```python
import numpy as np
import jax
import jax.numpy as jnp

def _softmax(x, axis=-1):
    return jax.nn.softmax(x, axis=axis)

def _gelu(x):
    return jax.nn.gelu(x, approximate=True)

def _silu(x):
    return jax.nn.silu(x)

def _sigmoid(x):
    return jax.nn.sigmoid(x)

def _layernorm(x, axis=-1, eps=1e-05):
    m = jnp.mean(x, axis=axis, keepdims=True)
    v = jnp.var(x, axis=axis, keepdims=True)
    return (x - m) / jnp.sqrt(v + eps)

def _scatter_add(tgt, idx, src, axis=0):
    return tgt.at[idx].add(src)

def _segment_sum(src, seg, n):
    return jax.ops.segment_sum(src, seg, n)
kernel_name = 'mk_lm_tower_d1_tok_ids512_r4_702f9e'

def setup_inputs(seed: int=0):
    np.random.seed(seed)
    _w = jnp.asarray

    def _rec_inputs():
        import jax
        import jax.numpy as jnp
        _rk = jax.random.key(seed)
        x = jax.random.randint(jax.random.fold_in(_rk, 1), (4, 512), 0, 32, jnp.int32)
        fside_BS_event_times = 49.562 + 29.0317 * jax.random.normal(jax.random.fold_in(_rk, 21), (4, 512), jnp.float32)
        mask_BS_i1_0 = jnp.where(jnp.ones((4, 512), dtype=bool), 1, 0).astype(jnp.int32)
        return (x, fside_BS_event_times, mask_BS_i1_0)
    x, fside_BS_event_times, mask_BS_i1_0 = _rec_inputs()

    def _L0_tok_setup():
        import jax, jax.numpy as jnp
        import numpy as np
        EPS = 1e-05
        NEG_INF = -1000000000.0

        def _layernorm(x, g, b):
            mu = x.mean(-1, keepdims=True)
            var = x.var(-1, keepdims=True)
            return (x - mu) / jnp.sqrt(var + EPS) * g + b

        def _time_encoding(t, d_model):
            i = jnp.arange(d_model)
            div_term = jnp.exp((2.0 * (i // 2)).astype(jnp.float32) * (-np.log(10000.0) / d_model))
            phase = t[..., None] * div_term
            return jnp.where(i % 2 == 0, jnp.sin(phase), jnp.cos(phase))
        key = jax.random.key(seed)
        B, S, D, H, L, V, PAD = (16, 256, 128, 4, 4, 32, 0)
        ks = jax.random.split(key, 12)
        event_times = jax.random.uniform(ks[0], (B, S), dtype=jnp.float32) * 100.0
        event_types = jax.random.randint(ks[1], (B, S), 0, V)
        non_pad_mask = jnp.ones((B, S), dtype=jnp.int32)
        type_emb = (jax.random.normal(ks[2], (V, D), dtype=jnp.float32) * 0.02).at[PAD].set(0.0)

        def w(k):
            return jax.random.normal(k, (H, L, D, D), dtype=jnp.float32) / np.sqrt(D)
        Wq, Wk, Wv, Wo = (w(ks[3]), w(ks[4]), w(ks[5]), w(ks[6]))
        zb = jnp.zeros((H, L, D), dtype=jnp.float32)
        return dict(event_types=event_types, event_times=event_times, non_pad_mask=non_pad_mask, type_emb=type_emb, Wq=Wq, bq=zb, Wk=Wk, bk=zb, Wv=Wv, bv=zb, Wo=Wo, bo=zb, ln_scale=jnp.ones((H, L, D), dtype=jnp.float32), ln_bias=zb, final_scale=jnp.ones((D,), dtype=jnp.float32), final_bias=jnp.zeros((D,), dtype=jnp.float32))
    _L0_tok_all = _L0_tok_setup()
    _L0_tok_in = {k: v for k, v in _L0_tok_all.items() if k in ('type_emb', 'Wq', 'bq', 'Wk', 'bk', 'Wv', 'bv', 'Wo', 'bo', 'ln_scale', 'ln_bias', 'final_scale', 'final_bias')}
    del _L0_tok_all

    def _L0_attn_setup():
        import jax, jax.numpy as jnp
        import numpy as np
        key = jax.random.key(seed)
        x = jax.random.normal(key, (4, 1024, 128), dtype=jnp.float32)
        return {'x': x}
    _L0_attn_all = _L0_attn_setup()
    _L0_attn_in = {k: v for k, v in _L0_attn_all.items() if k in ()}
    del _L0_attn_all

    def _L0_ffn_setup():
        import jax, jax.numpy as jnp
        import numpy as np
        CAPACITY_FACTOR = 1.2
        key = jax.random.key(seed)
        k1, k2, k3 = jax.random.split(key, 3)
        B, S, D, E = (8, 1024, 128, 16)
        x = jax.random.normal(k1, (B, S, D), dtype=jnp.float32)
        switch_w = jax.random.normal(k2, (E, D), dtype=jnp.float32) * 0.02
        switch_b = jnp.zeros((E,), dtype=jnp.float32)
        expert_w = jax.random.normal(k3, (E, D, D), dtype=jnp.float32) * 0.02
        expert_b = jnp.zeros((E, D), dtype=jnp.float32)
        return {'x': x, 'switch_w': switch_w, 'switch_b': switch_b, 'expert_w': expert_w, 'expert_b': expert_b}
    _L0_ffn_all = _L0_ffn_setup()
    _L0_ffn_in = {k: v for k, v in _L0_ffn_all.items() if k in ('switch_w', 'switch_b', 'expert_w', 'expert_b')}
    del _L0_ffn_all
    return {'x': x, 'fside_BS_event_times': fside_BS_event_times, 'mask_BS_i1_0': mask_BS_i1_0, 'L0_tok_type_emb': _L0_tok_in['type_emb'], 'L0_tok_Wq': _L0_tok_in['Wq'], 'L0_tok_bq': _L0_tok_in['bq'], 'L0_tok_Wk': _L0_tok_in['Wk'], 'L0_tok_bk': _L0_tok_in['bk'], 'L0_tok_Wv': _L0_tok_in['Wv'], 'L0_tok_bv': _L0_tok_in['bv'], 'L0_tok_Wo': _L0_tok_in['Wo'], 'L0_tok_bo': _L0_tok_in['bo'], 'L0_tok_ln_scale': _L0_tok_in['ln_scale'], 'L0_tok_ln_bias': _L0_tok_in['ln_bias'], 'L0_tok_final_scale': _L0_tok_in['final_scale'], 'L0_tok_final_bias': _L0_tok_in['final_bias'], 'L0_ffn_switch_w': _L0_ffn_in['switch_w'], 'L0_ffn_switch_b': _L0_ffn_in['switch_b'], 'L0_ffn_expert_w': _L0_ffn_in['expert_w'], 'L0_ffn_expert_b': _L0_ffn_in['expert_b']}

def reference(x, fside_BS_event_times, mask_BS_i1_0, L0_tok_type_emb, L0_tok_Wq, L0_tok_bq, L0_tok_Wk, L0_tok_bk, L0_tok_Wv, L0_tok_bv, L0_tok_Wo, L0_tok_bo, L0_tok_ln_scale, L0_tok_ln_bias, L0_tok_final_scale, L0_tok_final_bias, L0_ffn_switch_w, L0_ffn_switch_b, L0_ffn_expert_w, L0_ffn_expert_b):
    import jax
    import jax.numpy as jnp

    def _L0_tok_ref(event_types, event_times, non_pad_mask, type_emb, Wq, bq, Wk, bk, Wv, bv, Wo, bo, ln_scale, ln_bias, final_scale, final_bias):
        import jax, jax.numpy as jnp
        import numpy as np
        EPS = 1e-05
        NEG_INF = -1000000000.0

        def _layernorm(x, g, b):
            mu = x.mean(-1, keepdims=True)
            var = x.var(-1, keepdims=True)
            return (x - mu) / jnp.sqrt(var + EPS) * g + b

        def _time_encoding(t, d_model):
            i = jnp.arange(d_model)
            div_term = jnp.exp((2.0 * (i // 2)).astype(jnp.float32) * (-np.log(10000.0) / d_model))
            phase = t[..., None] * div_term
            return jnp.where(i % 2 == 0, jnp.sin(phase), jnp.cos(phase))
        D = type_emb.shape[1]
        L = Wq.shape[1]
        enc_input = _time_encoding(event_times, D) + type_emb[event_types]
        mask3 = non_pad_mask[:, None, :]
        scale = 1.0 / np.sqrt(D)

        def run_head(hp):
            wq, bq_, wk, bk_, wv, bv_, wo, bo_, g, b = hp
            x = enc_input
            for l in range(L):
                xn = _layernorm(x, g[l], b[l])
                q = xn @ wq[l] + bq_[l]
                k = xn @ wk[l] + bk_[l]
                v = xn @ wv[l] + bv_[l]
                scores = jnp.einsum('bqd,bkd->bqk', q, k) * scale
                scores = jnp.where(mask3 == 0, NEG_INF, scores)
                a = jax.nn.softmax(scores, axis=-1)
                o = jnp.einsum('bqk,bkd->bqd', a, v) @ wo[l] + bo_[l]
                x = x + o
            return x
        heads = jax.vmap(run_head)((Wq, bq, Wk, bk, Wv, bv, Wo, bo, ln_scale, ln_bias))
        return _layernorm(heads.mean(0), final_scale, final_bias)

    def _L0_attn_ref(x):
        import jax, jax.numpy as jnp
        import numpy as np
        raw_weights = jnp.einsum('btk,bsk->bts', x, x)
        weights = jax.nn.softmax(raw_weights, axis=2)
        y = jnp.einsum('bts,bsk->btk', weights, x)
        return y

    def _L0_ffn_ref(x, switch_w, switch_b, expert_w, expert_b):
        import jax, jax.numpy as jnp
        import numpy as np
        CAPACITY_FACTOR = 1.2
        B, S, D = x.shape
        E = switch_w.shape[0]
        N = B * S
        xf = x.reshape(N, D)
        logits = xf @ switch_w.T + switch_b
        probs = jax.nn.softmax(logits, axis=-1)
        route_probs = jnp.max(probs, axis=-1)
        routes = jnp.argmax(probs, axis=-1)
        oh = jax.nn.one_hot(routes, E, dtype=jnp.int32)
        pos = jnp.take_along_axis(jnp.cumsum(oh, axis=0), routes[:, None], axis=1)[:, 0] - 1
        capacity = int(CAPACITY_FACTOR * N / E)
        keep = pos < capacity
        buf = jnp.zeros((E, capacity, D), dtype=xf.dtype).at[routes, pos].set(xf)
        y = jnp.einsum('ecd,efd->ecf', buf, expert_w) + expert_b[:, None, :]
        gathered = y[routes, jnp.minimum(pos, capacity - 1)]
        out = jnp.where(keep[:, None], gathered, xf) * route_probs[:, None]
        return out.reshape(B, S, D)
    h = _L0_tok_ref(x, fside_BS_event_times, mask_BS_i1_0, L0_tok_type_emb, L0_tok_Wq, L0_tok_bq, L0_tok_Wk, L0_tok_bk, L0_tok_Wv, L0_tok_bv, L0_tok_Wo, L0_tok_bo, L0_tok_ln_scale, L0_tok_ln_bias, L0_tok_final_scale, L0_tok_final_bias)
    h = h + _L0_attn_ref(_layernorm(h, axis=-1))
    h = h + _L0_ffn_ref(_layernorm(h, axis=-1), L0_ffn_switch_w, L0_ffn_switch_b, L0_ffn_expert_w, L0_ffn_expert_b)
    return h

_drawn_inputs = setup_inputs


def setup_inputs(seed=0):
    import zlib

    import numpy as np

    out = dict(_drawn_inputs(seed))
    spreads = {'L0_tok_bq': (0.0, 0.421),
     'L0_tok_bk': (0.0, 0.8),
     'L0_tok_bv': (0.0, 0.1),
     'L0_tok_bo': (0.0, 0.1),
     'L0_tok_ln_scale': (1.0, 0.2),
     'L0_tok_ln_bias': (0.0, 0.1),
     'L0_tok_final_scale': (1.0, 0.2),
     'L0_tok_final_bias': (0.0, 0.1),
     'L0_ffn_switch_b': (0.0, 0.367),
     'L0_ffn_expert_b': (0.0, 0.8)}
    factors = {'L0_tok_type_emb': 4.087, 'L0_ffn_switch_w': 3.946, 'L0_ffn_expert_w': 8.0}
    for name, (base, spread) in spreads.items():
        noise = np.random.default_rng([zlib.crc32(name.encode()), seed]).standard_normal(out[name].shape)
        drawn = base * np.exp(spread * noise) if base else spread * noise
        out[name] = jnp.asarray(drawn.astype(out[name].dtype))
    for name, factor in factors.items():
        out[name] = (out[name] * factor).astype(out[name].dtype)
    return out
```

```python
from contextlib import ExitStack

import numpy as np

import concourse.bass as bass
from concourse import mybir

F32 = mybir.dt.float32
F32R = mybir.dt.float32r
BF16 = mybir.dt.bfloat16
I32 = mybir.dt.int32
U32 = mybir.dt.uint32
ALU = mybir.AluOpType
ACT = mybir.ActivationFunctionType
AX = mybir.AxisListType

P = 128
B, S = 4, 512
NC = S // P
NT = B * NC
H, L, V, E = 4, 4, 32, 16
NG = H * L
NU = NG * B
CAP = int(1.2 * B * S / E)
EPS = 1e-5
NEG = -1e9
SCALE = 1.0 / np.sqrt(P)
BIG = 1.5 * 2.0 ** 23
TWO_PI = 2.0 * np.pi
PI1 = 6.28125
PI2 = float(np.float32(np.round((TWO_PI - PI1) * 2 ** 20) / 2 ** 20))
PI3 = float(TWO_PI - PI1 - PI2)
PI_MAX = 3.1415925

ROW_BQ, ROW_BK, ROW_BV, ROW_LNB, ROW_SW, ROW_LNS, ROW_MASK, ROW_TIME = 0, 16, 32, 48, 64, 80, 96, 112
C_ID, C_FOLD, C_TRI, C_DIV, C_OFF, C_IOTA, C_END = 0, 128, 256, 384, 512, 640, 657


def shape_constants():
    c = np.zeros((P, C_END), np.float32)
    c[:, C_ID:C_ID + P] = np.eye(P)
    fold = np.eye(P)
    fold[0, 1:] = -1.0
    fold[:, 0] = 0.0
    c[:, C_FOLD:C_FOLD + P] = fold
    c[:, C_TRI:C_TRI + P] = np.triu(np.ones((P, P)))
    i = np.arange(P)
    rate = (2.0 * (i // 2)).astype(np.float32) * np.float32(-np.log(10000.0) / P)
    c[:, C_DIV:C_DIV + P] = np.exp(rate)
    c[:, C_OFF:C_OFF + P] = 0.25 * (i % 2)
    c[:, C_IOTA:C_IOTA + E] = np.arange(E)
    c[:, C_IOTA + E] = np.arange(P)
    return c


def tower(nc, ids, times, mask, type_emb, Wq, bq, Wk, bk, Wv, bv, Wo, bo, ln_scale, ln_bias,
          final_scale, final_bias, switch_w, switch_b, expert_w, expert_b, const, out):
    with ExitStack() as ctx:
        def sb(name, shape, dt=F32):
            return ctx.enter_context(nc.sbuf_tensor(name, shape, dt))

        def sem(name):
            return ctx.enter_context(nc.semaphore(name))

        bank = [ctx.enter_context(nc.psum_tensor(f"bank{i}", [P, 512], F32)) for i in range(8)]
        SC = bank[0:2]
        SA = bank[2:4]
        TB = bank[4]
        XB = bank[5]
        OB = [t[:, 0:258].rearrange("p (c d) -> p c d", c=2) for t in bank[6:8]]
        EMB = [bank[i] for i in (1, 2, 3, 7)]
        CUM = bank[2][:, 0:NT * E].rearrange("p (j e) -> p j e", e=E)

        K = sb("K", [P, C_END])
        ident = K[:, C_ID:C_ID + P]
        negident = sb("negident", [P, P], BF16)
        tri = sb("tri", [P, P], BF16)
        ones = sb("ones", [P, P], BF16)
        rows = sb("rows", [P, P])
        cols = sb("cols", [P, P])
        mask_i = sb("mask_i", [P, P], I32)
        mask_b = sb("mask_b", [P, B * S], I32)
        key_mask = sb("key_mask", [P, B, S])
        masked_all = sb("masked_all", [P, B])
        some_key = sb("some_key", [P, B])
        key_bias = sb("key_bias", [P, NT])
        fin_s = sb("fin_s", [P, P])
        fin_b = sb("fin_b", [P, P])
        sw_b = sb("sw_b", [P, 1])
        eb_rows = sb("eb_rows", [P, P])
        eb_cols = sb("eb_cols", [P, E])
        half = sb("half", [P, NC])
        eps_in = sb("eps_in", [P, NC])
        eps_sum = sb("eps_sum", [P, NC])
        ids_b = sb("ids_b", [V, B * S], I32)
        onehot = sb("onehot", [V, B * S])
        emb = sb("emb", [V, P])
        phase = sb("phase", [P, S])
        turns = sb("turns", [P, S])
        wave = sb("wave", [P, B, S])
        X = sb("X", [P, H, B, S])
        w_raw = sb("w_raw", [P, 4, P])
        bo_row = sb("bo_row", [1, P])
        fold_t = sb("fold_t", [P, P])
        lncol = sb("lncol", [P, 2])
        bias3 = sb("bias3", [P, 3])
        w_til = sb("w_til", [P, 3, P])
        g_hi = sb("g_hi", [P, P], F32R)
        g_lo = sb("g_lo", [P, P], F32R)
        wvo = sb("wvo", [P, P])
        stats = sb("stats", [P, NC, 6])
        mv = sb("mv", [P, NC, 2])
        veps = sb("veps", [P, NC])
        rstd = sb("rstd", [P, NC])
        z = [sb(f"z{i}", [P, NC, P]) for i in range(2)]
        zT = [sb(f"zT{i}", [P, S]) for i in range(4)]
        zh = [sb(f"zh{i}", [P, S], F32R) for i in range(4)]
        zl = [sb(f"zl{i}", [P, S], F32R) for i in range(4)]
        th = [sb(f"th{i}", [P, S], F32R) for i in range(2)]
        tl = [sb(f"tl{i}", [P, S], F32R) for i in range(2)]
        val = [sb(f"val{i}", [P, NC, P + 1]) for i in range(4)]
        mcol = sb("mcol", [P, NC], BF16)
        prob = [sb(f"prob{i}", [P, S]) for i in range(NC)]
        rsum = sb("rsum", [P, NC])
        h0 = sb("h0", [P, B, S])
        h1 = sb("h1", [P, NT, P])
        x3 = sb("x3", [P, NT, P])
        x3T = sb("x3T", [P, B * S])
        negsq = sb("negsq", [P, NC])
        logit = sb("logit", [P, NT, E])
        lexp = sb("lexp", [P, NT, E])
        top8 = sb("top8", [P, NT, 8])
        idx8 = sb("idx8", [P, NT, 8], U32)
        route1 = sb("route1", [P, NT, E], BF16)
        lsum = sb("lsum", [P, NT])
        rprob = sb("rprob", [P, NT])
        gate = sb("gate", [P, NT, E])
        kept = sb("kept", [P, NT])
        drop = sb("drop", [P, NT])
        ew = sb("ew", [P, E, P])
        ewT = sb("ewT", [P, E, P])
        acc = [sb(f"acc{i}", [P, P]) for i in range(2)]
        acc_out = [sb(f"acc_out{i}", [P, P]) for i in range(2)]

        ld_const, ld_rows, ld_mask, ld_tail, ld_w = map(sem, "ld_const ld_rows ld_mask ld_tail ld_w".split())
        stored = [sem("stored_even"), sem("stored_odd")]
        rows_ready, cols_t, cols_ready, eb_t, eb_ready = map(sem, "rows_ready cols_t cols_ready eb_t eb_ready".split())
        onehot_ready, emb_ready, angle_ready, wave_ready = map(sem, "onehot_ready emb_ready angle_ready wave_ready".split())
        x_ready, x_copied, mask_ready, setup = map(sem, "x_ready x_copied mask_ready setup".split())
        lncol_ready, fold_ready, w1_ready, w1_copied = map(sem, "lncol_ready fold_ready w1_ready w1_copied".split())
        bias3_ready, w_til_ready, w2_ready, w2_copied, w_ready = map(
            sem, "bias3_ready w_til_ready w2_ready w2_copied w_ready".split())
        stats_ready, mv_ready, veps_ready, rstd_ready, z_ready = map(
            sem, "stats_ready mv_ready veps_ready rstd_ready z_ready".split())
        zt_ready, zt_copied, zhi_ready, zlo_ready = map(sem, "zt_ready zt_copied zhi_ready zlo_ready".split())
        v_ready, v_copied, t_ready, th_ready = map(sem, "v_ready v_copied t_ready th_ready".split())
        sa_ready, max_ready, inj_ready, row_ready, tl_ready = map(
            sem, "sa_ready max_ready inj_ready row_ready tl_ready".split())
        sc_ready, exp_done, av_done, rsum_ready, x_updated = map(
            sem, "sc_ready exp_done av_done rsum_ready x_updated".split())
        ew_sub, ew_folded, ew_turned, ew_ready = map(sem, "ew_sub ew_folded ew_turned ew_ready".split())
        y_ready, y_turned, y_copied, tail_sc, tail_exp, tail_av = map(
            sem, "y_ready y_turned y_copied tail_sc tail_exp tail_av".split())
        x3_ready, x3_turned, x3_copied, logit_ready, lshift_ready, lexp_ready = map(
            sem, "x3_ready x3_turned x3_copied logit_ready lshift_ready lexp_ready".split())
        routed, cum_ready, expert_out, expert_used, acc_ready = map(
            sem, "routed cum_ready expert_out expert_used acc_ready".split())
        chain = sem("chain")
        passed = sem("passed")

        def unit(g, j, ahead):
            gg, b = g + (j + ahead) // B, (j + ahead) % B
            if isinstance(gg, int) and not 0 <= gg < NG:
                return None
            return gg, b, gg * B + b

        def next_pair(g):
            return None if isinstance(g, int) and g + 1 >= NG else g + 1

        def at_least(eng, s, n):
            if not isinstance(n, int) or n > 0:
                eng.wait_ge(s, n)

        def apart(eng, s, n):
            at_least(eng, s, n)
            if not isinstance(n, int):
                eng.sem_inc(passed, 1)

        def run_steps(step):
            def run(eng):
                for g in (-1, 0):
                    for j in range(B):
                        step(g, j)
                with eng.Fori(1, NG - 1) as g:
                    for j in range(B):
                        step(g, j)
                for j in range(B):
                    step(NG - 1, j)
                step(NG, 0)
            return run

        block = ctx.enter_context(nc.Block())

        @block.sync
        def _(sp):
            sp.dma_start(rows[ROW_TIME:ROW_TIME + NT, :],
                         times.rearrange("b (c p) -> (b c) p", p=P)).then_inc(ld_rows, 16)
            sp.dma_start(mask_i[ROW_MASK:ROW_MASK + NT, :],
                         mask.rearrange("b (c p) -> (b c) p", p=P)).then_inc(ld_rows, 16)
            sp.dma_start(rows[ROW_SW:ROW_SW + E, :], switch_w).then_inc(ld_rows, 16)
            sp.dma_start(sw_b[ROW_SW:ROW_SW + E, :], switch_b.rearrange("(e a) -> e a", a=1)).then_inc(ld_rows, 16)
            for a, at in ((bq, ROW_BQ), (bk, ROW_BK), (bv, ROW_BV), (ln_bias, ROW_LNB), (ln_scale, ROW_LNS)):
                for l in range(L):
                    sp.dma_start(rows[at + l * H:at + (l + 1) * H, :], a[:, l, :]).then_inc(ld_rows, 16)

            def step(g, j):
                gw = next_pair(g)
                if j == 0 and gw is not None:
                    at_least(sp, w_ready, gw)
                    i = (gw % H) * L + gw // H
                    for k, w in enumerate((Wq, Wk, Wv, Wo)):
                        v = w.rearrange("h l a b -> (h l) a b")
                        sp.dma_start(w_raw[:, k, :], v[bass.ds(i, 1), :, :].rearrange("o a b -> a (o b)")).then_inc(ld_w, 16)
                    sp.dma_start(bo_row[:, :], bo.rearrange("h l d -> (h l) d")[bass.ds(i, 1), :]).then_inc(ld_w, 16)
                if isinstance(g, int) and g == -1 and j == 0:
                    sp.dma_start(mask_b[:, :], mask.rearrange("b s -> (b s)").unsqueeze(0).to_broadcast([P, B * S])).then_inc(ld_mask, 16)
                    sp.dma_start(ew[:, :, :], expert_w.rearrange("e f d -> f e d")).then_inc(ld_tail, 16)
                    sp.dma_start(eb_rows[0:E, :], expert_b).then_inc(ld_tail, 16)
                    sp.dma_start(fin_s[:, :], final_scale.unsqueeze(0).to_broadcast([P, P])).then_inc(ld_tail, 16)
                    sp.dma_start(fin_b[:, :], final_bias.unsqueeze(0).to_broadcast([P, P])).then_inc(ld_tail, 16)

            run_steps(step)(sp)
            for j in range(NT):
                sp.wait_ge(acc_ready, j + 1)
                sp.dma_start(out.rearrange("b (c p) d -> (b c) p d", p=P)[j], acc_out[j % 2][:, :]).then_inc(stored[j % 2], 16)
            for s in stored:
                sp.wait_ge(s, 16 * NT // 2)

        @block.tensor
        def _(pe):
            pe.wait_ge(onehot_ready, 1)
            for b in range(B):
                for c in range(NC):
                    mm = pe.matmul(EMB[b][:, c * P:(c + 1) * P],
                                   onehot[:, (b * NC + c) * P:(b * NC + c + 1) * P], emb[:, :],
                                   start=True, stop=True)
                mm.then_inc(emb_ready, 1)
            pe.wait_ge(rows_ready, 2)
            pe.transpose(bank[0][:, 0:P], rows[:, :], ident).then_inc(cols_t, 1)
            pe.wait_ge(ld_tail, 64)
            pe.transpose(TB[:, 0:E], eb_rows[0:E, :], K[0:E, C_ID:C_ID + E]).then_inc(eb_t, 1)

            def scores(u, kc):
                g, b, n = u
                at_least(pe, exp_done, NC * n + kc - 1)
                if kc == 0:
                    at_least(pe, tl_ready, n + 1)
                    if isinstance(g, int) and n == 0:
                        pe.wait_ge(x_ready, B)
                ks = slice(kc * P, (kc + 1) * P)
                o = SC[kc % 2][:, :]
                pe.matmul(o, zh[b][:, ks], th[b % 2][:, :], start=True, stop=False)
                pe.matmul(o, zh[b][:, ks], tl[b % 2][:, :], start=False, stop=False)
                pe.matmul(o, zl[b][:, ks], th[b % 2][:, :], start=False, stop=True).then_inc(sc_ready, 1)

            def times_values(u, kc):
                g, b, n = u
                at_least(pe, exp_done, NC * n + kc + 1)
                if kc == 0:
                    at_least(pe, x_updated, n)
                for c in range(NC):
                    mm = pe.matmul(OB[c // 2][:, c % 2, :], prob[kc][:, c * P:(c + 1) * P],
                                   val[b][:, kc, :], start=(kc == 0 and c % 2 == 0), stop=(kc == NC - 1),
                                   skip_group_check=True)
                mm.then_inc(av_done, 1)

            def rough_scores(u, c):
                g, b, n = u
                if c == 0:
                    at_least(pe, th_ready, n + 1)
                    if isinstance(g, int) and n == 0:
                        pe.wait_ge(x_ready, 3)
                at_least(pe, max_ready, NC * n + c - 1)
                pe.matmul(SA[c % 2][:, :], th[b % 2][:, c * P:(c + 1) * P], zh[b][:, :],
                          start=True, stop=True).then_inc(sa_ready, 1)

            def turn_z(u):
                g, b, n = u
                at_least(pe, z_ready, n + 1)
                at_least(pe, v_copied, n)
                for c in range(NC):
                    mm = pe.transpose(XB[:, c * P:(c + 1) * P], z[b % 2][:, c, :], ident)
                mm.then_inc(zt_ready, 1)

            def values(u):
                g, b, n = u
                at_least(pe, zt_copied, n + 1)
                at_least(pe, w_ready, g + 1)
                for c in range(NC):
                    mm = pe.matmul(XB[:, c * P:(c + 1) * P], zT[b][:, c * P:(c + 1) * P], wvo[:, :],
                                   start=True, stop=True)
                mm.then_inc(v_ready, 1)

            def project(u):
                g, b, n = u
                at_least(pe, zlo_ready, n + 1)
                at_least(pe, tl_ready, n)
                pe.matmul(TB[:, :], g_hi[:, :], zh[b][:, :], start=True, stop=False)
                pe.matmul(TB[:, :], g_hi[:, :], zl[b][:, :], start=False, stop=False)
                pe.matmul(TB[:, :], g_lo[:, :], zh[b][:, :], start=False, stop=True).then_inc(t_ready, 1)

            def inject(u):
                g, b, n = u
                at_least(pe, max_ready, NC * (n + 1))
                for c in range(NC):
                    mm = pe.matmul(TB[0:1, c * P:(c + 1) * P], mcol[:, c:c + 1], negident[:, :],
                                   start=False, stop=True, skip_group_check=True)
                mm.then_inc(inj_ready, 1)

            def fold_1(gw, n2):
                at_least(pe, fold_ready, gw + 1)
                at_least(pe, ld_w, 80 * (gw + 1))
                if n2:
                    at_least(pe, zt_copied, n2[2] + 1)
                for k in range(3):
                    mm = pe.matmul(XB[:, k * P:(k + 1) * P], w_raw[:, k, :], fold_t[:, :], start=True, stop=True)
                mm.then_inc(w1_ready, 1)

            def fold_2(gw, n2):
                at_least(pe, w_til_ready, gw + 1)
                if n2:
                    at_least(pe, zt_copied, n2[2] + 1)
                pe.matmul(XB[:, 0:P], w_til[:, 0, :], w_til[:, 1, :], start=True, stop=True)
                pe.matmul(XB[:, P:2 * P], w_til[:, 2, :], w_raw[:, 3, :], start=True, stop=True).then_inc(w2_ready, 1)

            def step(g, j):
                last, now, nxt, nxt2 = (unit(g, j, a) for a in (-1, 0, 1, 2))
                gw = next_pair(g)
                if now: scores(now, 0)
                if last: times_values(last, 2)
                if nxt: rough_scores(nxt, 0)
                if nxt2 and isinstance(g, int) and nxt2[2] == 0:
                    pe.wait_ge(w1_copied, 1)
                if nxt2: turn_z(nxt2)
                if nxt: rough_scores(nxt, 1)
                if last: times_values(last, 3)
                if now: scores(now, 1)
                if nxt: rough_scores(nxt, 2)
                if j == 1 and gw is not None:
                    at_least(pe, v_copied, gw * B - 1)
                    fold_1(gw, nxt2)
                if j == 2 and gw is not None: fold_2(gw, nxt2)
                if nxt: rough_scores(nxt, 3)
                if now: scores(now, 2)
                if nxt2:
                    if j == 1 and gw is not None:
                        at_least(pe, w1_copied, g + 2)
                    values(nxt2)
                if nxt: inject(nxt)
                if now: times_values(now, 0)
                if now: scores(now, 3)
                if now: times_values(now, 1)
                if nxt2: project(nxt2)

            run_steps(step)(pe)

            pe.wait_ge(ew_folded, 1)
            for q in range(4):
                if q >= 2:
                    pe.wait_ge(ew_ready, q - 1)
                for k in range(4):
                    mm = pe.transpose(SA[q % 2][:, k * P:(k + 1) * P], ew[:, 4 * q + k, :], ident)
                mm.then_inc(ew_turned, 1)

            def tail_values(b, kc):
                pe.wait_ge(tail_exp, NC * b + kc + 1)
                for c in range(NC):
                    mm = pe.matmul(OB[c // 2][:, c % 2, :], prob[kc][:, c * P:(c + 1) * P], val[0][:, kc, :],
                                   start=(kc == 0 and c % 2 == 0), stop=(kc == NC - 1), skip_group_check=True)
                if kc == NC - 1:
                    mm.then_inc(tail_av, 1)

            for b in range(B):
                pe.wait_ge(y_ready, b + 1)
                for c in range(NC):
                    mm = pe.transpose(XB[:, c * P:(c + 1) * P], z[0][:, c, :], ident)
                mm.then_inc(y_turned, 1)
                for c in range(NC):
                    mm = pe.transpose(TB[:, c * P:(c + 1) * P], z[1][:, c, :], ident)
                mm.then_inc(y_turned, 1)
                pe.wait_ge(y_copied, 2 * b + 2)
                for kc in range(NC):
                    if kc >= 2:
                        pe.wait_ge(tail_exp, NC * b + kc - 1)
                    pe.matmul(SC[kc % 2][:, :], zT[0][:, kc * P:(kc + 1) * P], zT[1][:, :],
                              start=True, stop=True).then_inc(tail_sc, 1)
                    if kc:
                        tail_values(b, kc - 1)
                tail_values(b, NC - 1)
                pe.wait_ge(x3_ready, b + 1)
                for c in range(NC):
                    mm = pe.transpose(XB[:, c * P:(c + 1) * P], z[0][:, c, :], ident)
                mm.then_inc(x3_turned, 1)
                pe.wait_ge(x3_copied, b + 1)
                for c in range(NC):
                    mm = pe.matmul(bank[3][:, c * E:(c + 1) * E], x3T[:, (b * NC + c) * P:(b * NC + c + 1) * P],
                                   cols[:, ROW_SW:ROW_SW + E], start=True, stop=True)
                mm.then_inc(logit_ready, 1)
            pe.wait_ge(routed, B)
            pe.matmul(CUM, tri[:, :], route1[:, :, :], start=True, stop=True)
            for i in range(NT - 1):
                mm = pe.matmul(CUM[:, i + 1:NT, :], ones[:, :],
                               route1[:, i:i + 1, :].to_broadcast([P, NT - 1 - i, E]),
                               start=False, stop=True, skip_group_check=True)
            mm.then_inc(cum_ready, 1)
            for j in range(NT):
                for q in range(4):
                    at_least(pe, expert_used, 4 * j + q - 1)
                    pe.matmul(SC[q % 2][:, :], x3T[:, j * P:(j + 1) * P],
                              ewT[:, 4 * q:4 * q + 4, :], start=True, stop=True).then_inc(expert_out, 1)

        @block.scalar
        def _(act):
            act.dma_start(K[:, :], const).then_inc(ld_const, 16)
            act.dma_start(ids_b[:, :], ids.rearrange("b s -> (b s)").unsqueeze(0).to_broadcast([V, B * S])).then_inc(ld_const, 16)
            act.dma_start(emb[:, :], type_emb).then_inc(ld_const, 16)
            act.wait_ge(cols_t, 1)
            act.copy(cols[:, :], bank[0][:, 0:P]).then_inc(cols_ready, 1)
            act.wait_ge(eb_t, 1)
            act.copy(eb_cols[:, :], TB[:, 0:E]).then_inc(eb_ready, 1)
            for b in range(B):
                act.wait_ge(angle_ready, b + 1)
                act.activation(wave[:, b, :], wave[:, b, :], ACT.Sin).then_inc(wave_ready, 1)

            def exps(u, kc):
                g, b, n = u
                at_least(act, sc_ready, NC * n + kc + 1)
                at_least(act, av_done, NC * (n - 1) + kc + 1)
                act.activation(prob[kc][:, :], SC[kc % 2][:, :], ACT.Exp,
                               bias=key_bias[:, b * NC + kc:b * NC + kc + 1]).then_inc(exp_done, 1)

            def step(g, j):
                now, nxt, nxt2 = (unit(g, j, a) for a in (0, 1, 2))
                gw = next_pair(g)
                if now: exps(now, 0)
                if nxt2:
                    at_least(act, zt_ready, nxt2[2] + 1)
                    act.copy(zT[nxt2[1]][:, :], XB[:, :]).then_inc(zt_copied, 1)
                if now: exps(now, 1)
                if j == 1 and gw is not None:
                    at_least(act, w1_ready, gw + 1)
                    act.copy(w_til[:, :, :], XB[:, 0:3 * P].rearrange("p (k d) -> p k d", k=3)).then_inc(w1_copied, 1)
                if j == 2 and gw is not None:
                    at_least(act, w2_ready, gw + 1)
                    act.activation(g_hi[:, :], XB[:, 0:P], ACT.Identity, scale=float(SCALE)).then_inc(w2_copied, 1)
                    act.copy(wvo[:, :], XB[:, P:2 * P]).then_inc(w2_copied, 1)
                if now: exps(now, 2)
                if nxt2:
                    at_least(act, v_ready, nxt2[2] + 1)
                    act.copy(val[nxt2[1]][:, :, 0:P], XB[:, :].rearrange("p (c d) -> p c d", c=NC)).then_inc(v_copied, 1)
                if nxt:
                    at_least(act, inj_ready, nxt[2] + 1)
                    act.activation(th[nxt[1] % 2][0:1, :], TB[0:1, :], ACT.Identity,
                                   scale=some_key[0:1, nxt[1]:nxt[1] + 1]).then_inc(row_ready, 1)
                if now: exps(now, 3)
                if nxt2:
                    at_least(act, t_ready, nxt2[2] + 1)
                    act.activation(th[nxt2[1] % 2][:, :], TB[:, :], ACT.Identity,
                                   scale=some_key[:, nxt2[1]:nxt2[1] + 1]).then_inc(th_ready, 1)

            act.wait_ge(mask_ready, 1)
            run_steps(step)(act)

            for q in range(4):
                act.wait_ge(ew_turned, q + 1)
                act.copy(ewT[:, 4 * q:4 * q + 4, :], SA[q % 2][:, :].rearrange("p (k d) -> p k d", k=4)).then_inc(ew_ready, 1)
            for b in range(B):
                act.wait_ge(y_turned, 2 * b + 1)
                act.copy(zT[0][:, :], XB[:, :]).then_inc(y_copied, 1)
                act.wait_ge(y_turned, 2 * b + 2)
                act.copy(zT[1][:, :], TB[:, :]).then_inc(y_copied, 1)
                for kc in range(NC):
                    act.wait_ge(tail_sc, NC * b + kc + 1)
                    act.activation(prob[kc][:, :], SC[kc % 2][:, :], ACT.Exp).then_inc(tail_exp, 1)
                act.wait_ge(x3_turned, b + 1)
                act.copy(x3T[:, b * S:(b + 1) * S], XB[:, :]).then_inc(x3_copied, 1)
                act.wait_ge(lshift_ready, b + 1)
                js = slice(b * NC, (b + 1) * NC)
                act.activation(lexp[:, js, :], lexp[:, js, :], ACT.Exp).then_inc(lexp_ready, 1)

        @block.vector
        def _(dve):
            count = [0]

            def then(ins):
                count[0] += 1
                ins.then_inc(chain, 1)
                dve.wait_ge(chain, count[0])

            for t in z:
                dve.memset(t[:, :, 0:1], 1.0)
            for t in val:
                dve.memset(t[:, :, P:P + 1], 1.0)
            dve.memset(half[:, :], -0.5)
            dve.memset(eps_in[:, :], EPS)
            dve.memset(eps_sum[:, :], H * H * EPS)
            dve.memset(ones[:, :], 1.0)
            dve.wait_ge(ld_const, 48)
            dve.tensor_scalar(onehot[:, :], ids_b[:, :], K[0:V, C_IOTA + E:C_IOTA + E + 1], None,
                              ALU.is_equal).then_inc(onehot_ready, 1)
            dve.wait_ge(ld_rows, 16 * 24)
            sw_rows = rows[ROW_SW:ROW_SW + E, :]
            then(dve.tensor_scalar(sw_rows[:, 1:P], sw_rows[:, 1:P], sw_rows[:, 0:1], None, ALU.subtract))
            dve.tensor_copy(sw_rows[:, 0:1], sw_b[ROW_SW:ROW_SW + E, :]).then_inc(rows_ready, 1)
            dve.tensor_scalar(rows[ROW_MASK:ROW_MASK + NT, :], mask_i[ROW_MASK:ROW_MASK + NT, :], 0, NEG,
                              ALU.is_equal, ALU.mult).then_inc(rows_ready, 1)
            dve.tensor_copy(tri[:, :], K[:, C_TRI:C_TRI + P])
            dve.tensor_scalar(negident[:, :], ident, -1.0, None, ALU.mult).then_inc(setup, 1)

            def encode(b):
                tcol = cols[:, ROW_TIME + b * NC:ROW_TIME + (b + 1) * NC]
                ph = phase[:, :].rearrange("p (c d) -> p c d", c=NC)
                div = K[:, C_DIV:C_DIV + P].unsqueeze(1).to_broadcast([P, NC, P])
                off = K[:, C_OFF:C_OFF + P].unsqueeze(1).to_broadcast([P, NC, P])
                tu = turns[:, :].rearrange("p (c d) -> p c d", c=NC)
                an = wave[:, b, :].rearrange("p (c d) -> p c d", c=NC)
                then(dve.tensor_tensor(ph, tcol.unsqueeze(2).to_broadcast([P, NC, P]), div, ALU.mult))
                then(dve.scalar_tensor_tensor(out=tu, in0=ph, scalar=float(1.0 / TWO_PI), in1=off, op0=ALU.mult, op1=ALU.add))
                then(dve.tensor_scalar(turns[:, :], turns[:, :], BIG, BIG, ALU.add, ALU.subtract))
                then(dve.scalar_tensor_tensor(out=ph, in0=tu, scalar=-PI1, in1=ph, op0=ALU.mult, op1=ALU.add))
                then(dve.scalar_tensor_tensor(out=ph, in0=tu, scalar=-PI2, in1=ph, op0=ALU.mult, op1=ALU.add))
                then(dve.scalar_tensor_tensor(out=ph, in0=tu, scalar=-PI3, in1=ph, op0=ALU.mult, op1=ALU.add))
                then(dve.scalar_tensor_tensor(out=an, in0=off, scalar=TWO_PI, in1=ph, op0=ALU.mult, op1=ALU.add))
                dve.tensor_scalar(wave[:, b, :], wave[:, b, :], PI_MAX, -PI_MAX, ALU.min, ALU.max).then_inc(angle_ready, 1)

            dve.wait_ge(cols_ready, 1)
            for b in range(B):
                encode(b)
            dve.wait_ge(ld_mask, 16)
            then(dve.tensor_scalar(key_mask[:, :, :].rearrange("p b s -> p (b s)"), mask_b[:, :], 0, NEG, ALU.is_equal, ALU.mult))
            then(dve.tensor_reduce(masked_all[:, :], key_mask[:, :, :], AX.X, ALU.max))
            then(dve.tensor_scalar(some_key[:, :], masked_all[:, :], 0.0, None, ALU.is_equal))
            for b in range(B):
                dve.tensor_scalar(key_mask[:, b, :], key_mask[:, b, :], some_key[:, b:b + 1], None, ALU.mult)
            dve.tensor_tensor(key_bias[:, :].rearrange("p (b c) -> p b c", b=B),
                              cols[:, ROW_MASK:ROW_MASK + NT].rearrange("p (b c) -> p b c", b=B),
                              some_key[:, :].unsqueeze(2).to_broadcast([P, B, NC]), ALU.mult).then_inc(mask_ready, 1)
            dve.wait_ge(mask_ready, 1)

            def maxima(u, c):
                g, b, n = u
                if c == 0:
                    apart(dve, inj_ready, n)
                apart(dve, sa_ready, NC * n + c + 1)
                sa = SA[c % 2][:, :]
                dve.tensor_tensor_reduce(out=sa, in0=sa, in1=key_mask[:, b, :], scale=1.0, scalar=-3e38,
                                         op0=ALU.add, op1=ALU.max, accum_out=mcol[:, c:c + 1]).then_inc(max_ready, 1)

            def row_stats(x, n):
                for c in range(NC):
                    ins = dve.bn_stats(stats[:, c, :], x[:, c * P:(c + 1) * P])
                ins.then_inc(stats_ready, 1)
                apart(dve, rstd_ready, n)
                apart(dve, stats_ready, n + 1)
                for c in range(NC):
                    ins = dve.bn_aggr(mv[:, c, :], stats[:, c, :])
                ins.then_inc(mv_ready, 1)

            def step(g, j):
                last, now, nxt, nxt2, nxt3 = (unit(g, j, a) for a in (-1, 0, 1, 2, 3))
                gw = next_pair(g)
                if nxt3 and nxt3[2] is not None and isinstance(nxt3[0], int) and nxt3[0] == 0:
                    b = nxt3[1]
                    dve.wait_ge(wave_ready, b + 1)
                    dve.wait_ge(emb_ready, b + 1)
                    dve.tensor_tensor(X[:, 0, b, :], wave[:, b, :], EMB[b][:, :], ALU.add).then_inc(x_ready, 1)
                    dve.wait_ge(x_ready, b + 1)
                if isinstance(g, int) and g == 0 and j:
                    dve.wait_ge(x_copied, B if j == 3 else j)
                if nxt: maxima(nxt, 0)
                if nxt3:
                    row_stats(X[:, nxt3[0] % H, nxt3[1], :], nxt3[2])
                if nxt: maxima(nxt, 1)
                if last:
                    g_, b_, n_ = last
                    at_least(dve, av_done, NC * (n_ + 1))
                    dve.reciprocal(rsum[:, 0:2], OB[0][:, :, P])
                    dve.reciprocal(rsum[:, 2:4], OB[1][:, :, P]).then_inc(rsum_ready, 1)
                    at_least(dve, rsum_ready, n_ + 1)
                    for c in range(NC):
                        xs = X[:, g_ % H, b_, c * P:(c + 1) * P]
                        ins = dve.scalar_tensor_tensor(out=xs, in0=OB[c // 2][:, c % 2, 0:P], scalar=rsum[:, c:c + 1],
                                                       in1=xs, op0=ALU.mult, op1=ALU.add)
                    ins.then_inc(x_updated, 1)
                if j == 2 and gw is not None:
                    at_least(dve, w2_copied, 2 * (gw + 1))
                    dve.scalar_tensor_tensor(out=g_lo[:, :], in0=XB[:, 0:P], scalar=float(SCALE), in1=g_hi[:, :].bitcast(F32),
                                             op0=ALU.mult, op1=ALU.subtract)
                    dve.tensor_tensor(wvo[0:1, :], wvo[0:1, :], bo_row[:, :], ALU.add).then_inc(w_ready, 1)
                if nxt: maxima(nxt, 2)
                if nxt: maxima(nxt, 3)
                if nxt2:
                    at_least(dve, zhi_ready, nxt2[2] + 1)
                    dve.tensor_tensor(zl[nxt2[1]][:, :], zT[nxt2[1]][:, :], zh[nxt2[1]][:, :].bitcast(F32),
                                      ALU.subtract).then_inc(zlo_ready, 1)
                if nxt:
                    at_least(dve, row_ready, nxt[2] + 1)
                    t = nxt[1] % 2
                    dve.scalar_tensor_tensor(out=tl[t][:, :], in0=TB[:, :], scalar=some_key[:, nxt[1]:nxt[1] + 1],
                                             in1=th[t][:, :].bitcast(F32), op0=ALU.mult, op1=ALU.subtract).then_inc(tl_ready, 1)
                if nxt3:
                    at_least(dve, rstd_ready, nxt3[2] + 1)
                    at_least(dve, zt_ready, nxt3[2] - 1)
                    for c in range(NC):
                        ins = dve.tensor_scalar(z[nxt3[1] % 2][:, c, 1:P], X[:, nxt3[0] % H, nxt3[1], c * P + 1:(c + 1) * P],
                                                mv[:, c, 0:1], rstd[:, c:c + 1], ALU.subtract, ALU.mult)
                    ins.then_inc(z_ready, 1)

            run_steps(step)(dve)

            ln = [NU]

            def tail_stats(x):
                row_stats(x, ln[0])
                ln[0] += 1
                dve.wait_ge(rstd_ready, ln[0])

            def normalised(out_, x, c):
                return dve.tensor_scalar(out_, x, mv[:, c, 0:1], rstd[:, c:c + 1], ALU.subtract, ALU.mult)

            dve.wait_ge(x_updated, NU)
            dve.wait_ge(ld_tail, 64)
            for b in range(B):
                hb = h0[:, b, :]
                h3 = hb.rearrange("p (c d) -> p c d", c=NC)
                js = slice(b * NC, (b + 1) * NC)
                then(dve.tensor_tensor(hb, X[:, 0, b, :], X[:, 1, b, :], ALU.add))
                then(dve.tensor_tensor(hb, hb, X[:, 2, b, :], ALU.add))
                then(dve.tensor_tensor(hb, hb, X[:, 3, b, :], ALU.add))
                tail_stats(hb)
                for c in range(NC):
                    ins = normalised(h3[:, c, :], h3[:, c, :], c)
                then(ins)
                then(dve.tensor_tensor(h3, h3, fin_s[:, :].unsqueeze(1).to_broadcast([P, NC, P]), ALU.mult))
                then(dve.tensor_tensor(h3, h3, fin_b[:, :].unsqueeze(1).to_broadcast([P, NC, P]), ALU.add))
                tail_stats(hb)
                for c in range(NC):
                    ins = normalised(val[0][:, c, 0:P], h3[:, c, :], c)
                then(ins)
                then(dve.tensor_tensor(negsq[:, :], mv[:, :, 1], rstd[:, :], ALU.mult))
                then(dve.tensor_tensor(negsq[:, :], negsq[:, :], rstd[:, :], ALU.mult))
                dve.tensor_scalar(z[1][:, :, 0], negsq[:, :], -float(P), None, ALU.mult)
                dve.tensor_copy(z[0][:, :, 1:P], val[0][:, :, 1:P])
                for c in range(NC):
                    ins = dve.tensor_scalar(z[1][:, c, 1:P], val[0][:, c, 1:P], val[0][:, c, 0:1], None, ALU.subtract)
                ins.then_inc(y_ready, 1)
                dve.wait_ge(tail_av, b + 1)
                dve.reciprocal(rsum[:, 0:2], OB[0][:, :, P])
                then(dve.reciprocal(rsum[:, 2:4], OB[1][:, :, P]))
                for c in range(NC):
                    ins = dve.scalar_tensor_tensor(out=h1[:, b * NC + c, :], in0=OB[c // 2][:, c % 2, 0:P], scalar=rsum[:, c:c + 1],
                                                   in1=h3[:, c, :], op0=ALU.mult, op1=ALU.add)
                then(ins)
                tail_stats(h1[:, js, :].rearrange("p c d -> p (c d)"))
                for c in range(NC):
                    ins = normalised(x3[:, b * NC + c, :], h1[:, b * NC + c, :], c)
                then(ins)
                dve.tensor_copy(z[0][:, :, 1:P], x3[:, js, 1:P]).then_inc(x3_ready, 1)
                dve.wait_ge(logit_ready, b + 1)
                then(dve.tensor_copy(logit[:, js, :], bank[3][:, 0:NC * E].rearrange("p (c e) -> p c e", e=E)))
                for c in range(NC):
                    ins = dve.max(top8[:, b * NC + c, :], logit[:, b * NC + c, :])
                then(ins)
                for c in range(NC):
                    ins = dve.max_index(idx8[:, b * NC + c, :], top8[:, b * NC + c, :], logit[:, b * NC + c, :])
                then(ins)
                dve.tensor_tensor(lexp[:, js, :], logit[:, js, :], top8[:, js, 0:1].to_broadcast([P, NC, E]),
                                  ALU.subtract).then_inc(lshift_ready, 1)
                dve.tensor_tensor(route1[:, js, :], K[:, C_IOTA:C_IOTA + E].unsqueeze(1).to_broadcast([P, NC, E]),
                                  idx8[:, js, 0:1].to_broadcast([P, NC, E]), ALU.is_equal).then_inc(routed, 1)
                dve.wait_ge(lexp_ready, b + 1)
                then(dve.tensor_reduce(lsum[:, js], lexp[:, js, :], AX.X, ALU.add))
                then(dve.reciprocal(rprob[:, js], lsum[:, js]))
            dve.wait_ge(cum_ready, 1)
            dve.wait_ge(routed, B)
            then(dve.scalar_tensor_tensor(out=gate[:, :, :], in0=CUM, scalar=float(CAP) + 0.5, in1=route1[:, :, :],
                                          op0=ALU.is_le, op1=ALU.mult))
            then(dve.tensor_reduce(kept[:, :], gate[:, :, :], AX.X, ALU.add))
            then(dve.tensor_scalar(drop[:, :], kept[:, :], -1.0, 1.0, ALU.mult, ALU.add))
            then(dve.tensor_tensor(drop[:, :], drop[:, :], rprob[:, :], ALU.mult))
            then(dve.tensor_tensor(gate[:, :, :], gate[:, :, :], rprob[:, :].unsqueeze(2).to_broadcast([P, NT, E]), ALU.mult))
            for j in range(NT):
                a = acc[j % 2][:, :]
                if j >= 2:
                    dve.wait_ge(stored[j % 2], 16 * (j // 2))
                then(dve.scalar_tensor_tensor(out=a, in0=x3[:, j, :], scalar=drop[:, j:j + 1], in1=h1[:, j, :],
                                              op0=ALU.mult, op1=ALU.add))
                for q in range(4):
                    dve.wait_ge(expert_out, 4 * j + q + 1)
                    for k in range(4):
                        ins = dve.scalar_tensor_tensor(out=a, in0=SC[q % 2][:, k * P:(k + 1) * P],
                                                       scalar=gate[:, j, 4 * q + k:4 * q + k + 1], in1=a,
                                                       op0=ALU.mult, op1=ALU.add)
                        if k < 3:
                            then(ins)
                    ins.then_inc(expert_used, 1)
                    dve.wait_ge(expert_used, 4 * j + q + 1)
                dve.tensor_copy(acc_out[j % 2][:, :], a).then_inc(acc_ready, 1)

        @block.gpsimd
        def _(pool):
            def fold_matrix(gw):
                pool.tensor_copy(lncol[:, 0:1], cols[:, bass.ds(ROW_LNS + gw, 1)])
                pool.tensor_copy(lncol[:, 1:2], cols[:, bass.ds(ROW_LNB + gw, 1)]).then_inc(lncol_ready, 1)
                apart(pool, w1_ready, gw)
                apart(pool, lncol_ready, gw + 1)
                pool.tensor_scalar(fold_t[:, 1:P], K[:, C_FOLD + 1:C_FOLD + P], lncol[:, 0:1], None, ALU.mult)
                pool.tensor_copy(fold_t[:, 0:1], lncol[:, 1:2]).then_inc(fold_ready, 1)

            def normaliser(n, eps):
                at_least(pool, mv_ready, n + 1)
                pool.tensor_tensor(veps[:, :], mv[:, :, 1], eps[:, :], ALU.add).then_inc(veps_ready, 1)
                at_least(pool, veps_ready, n + 1)
                at_least(pool, z_ready, n)
                pool.tensor_tensor(rstd[:, :], veps[:, :], half[:, :], ALU.pow).then_inc(rstd_ready, 1)

            def step(g, j):
                now, nxt2, nxt3 = (unit(g, j, a) for a in (0, 2, 3))
                gw = next_pair(g)
                if j == 0 and gw is not None:
                    fold_matrix(gw)
                if nxt3:
                    normaliser(nxt3[2], eps_in)
                if isinstance(g, int) and nxt3 and nxt3[0] == 0:
                    b = nxt3[1]
                    pool.wait_ge(x_ready, b + 1)
                    for h in range(1, H):
                        ins = pool.tensor_copy(X[:, h, b, :], X[:, 0, b, :])
                    ins.then_inc(x_copied, 1)
                if nxt2:
                    apart(pool, zt_copied, nxt2[2] + 1)
                    pool.tensor_copy(zh[nxt2[1]][:, :], zT[nxt2[1]][:, :]).then_inc(zhi_ready, 1)
                if j == 1 and gw is not None:
                    pool.tensor_copy(bias3[:, :], cols[:, 0:3 * NG].rearrange("p (k g) -> p g k", k=3)[:, bass.ds(gw, 1), :]
                                     .rearrange("p o k -> p (o k)")).then_inc(bias3_ready, 1)
                    at_least(pool, bias3_ready, gw + 1)
                    at_least(pool, w1_copied, gw + 1)
                    pool.tensor_tensor(w_til[:, :, 0], w_til[:, :, 0], bias3[:, :], ALU.add).then_inc(w_til_ready, 1)
                if isinstance(g, int) and g == 0 and j == 2:
                    pool.wait_ge(ld_tail, 64)
                    pool.wait_ge(eb_ready, 1)
                    pool.tensor_tensor(ew[:, :, 1:P], ew[:, :, 1:P], ew[:, :, 0:1].to_broadcast([P, E, P - 1]),
                                       ALU.subtract).then_inc(ew_sub, 1)
                    pool.wait_ge(ew_sub, 1)
                    pool.tensor_copy(ew[:, :, 0], eb_cols[:, :]).then_inc(ew_folded, 1)

            pool.wait_ge(setup, 1)
            pool.wait_ge(cols_ready, 1)
            run_steps(step)(pool)
            for b in range(B):
                for i, eps in enumerate((eps_sum, eps_in, eps_in)):
                    n = NU + 3 * b + i
                    pool.wait_ge(mv_ready, n + 1)
                    pool.tensor_tensor(veps[:, :], mv[:, :, 1], eps[:, :], ALU.add).then_inc(veps_ready, 1)
                    pool.wait_ge(veps_ready, n + 1)
                    pool.tensor_tensor(rstd[:, :], veps[:, :], half[:, :], ALU.pow).then_inc(rstd_ready, 1)


_INS = ["x", "fside_BS_event_times", "mask_BS_i1_0", "L0_tok_type_emb", "L0_tok_Wq", "L0_tok_bq", "L0_tok_Wk",
        "L0_tok_bk", "L0_tok_Wv", "L0_tok_bv", "L0_tok_Wo", "L0_tok_bo", "L0_tok_ln_scale", "L0_tok_ln_bias",
        "L0_tok_final_scale", "L0_tok_final_bias", "L0_ffn_switch_w", "L0_ffn_switch_b", "L0_ffn_expert_w",
        "L0_ffn_expert_b"]


def kernel(**inputs):
    import concourse.bacc as bacc
    from concourse.bass_utils import run_bass_kernel_spmd

    nc = bacc.Bacc("TRN2", target_bir_lowering=False, num_devices=1)
    arrays, args = {}, []
    for name in _INS:
        a = np.ascontiguousarray(inputs[name])
        arrays[f"in_{name}"] = a
        args.append(nc.dram_tensor(f"in_{name}", a.shape, mybir.dt.from_np(a.dtype), kind="ExternalInput").ap())
    const = shape_constants()
    arrays["in_const"] = const
    args.append(nc.dram_tensor("in_const", const.shape, F32, kind="ExternalInput").ap())
    args.append(nc.dram_tensor("out_h", (B, S, P), F32, kind="ExternalOutput").ap())
    tower(nc, *args)
    r = run_bass_kernel_spmd(nc, [arrays], core_ids=[0])
    return r.results[0]["out_h"]
```

```python
from contextlib import ExitStack

import numpy as np

import concourse.bass as bass
from concourse import mybir

F32 = mybir.dt.float32
F32R = mybir.dt.float32r
BF16 = mybir.dt.bfloat16
I32 = mybir.dt.int32
U32 = mybir.dt.uint32
ALU = mybir.AluOpType
ACT = mybir.ActivationFunctionType
AX = mybir.AxisListType

P = 128
B, S = 4, 512
NC = S // P
NT = B * NC
H, L, V, E = 4, 4, 32, 16
NG = H * L
NU = NG * B
CAP = int(1.2 * B * S / E)
EPS = 1e-5
NEG = -1e9
SCALE = 1.0 / np.sqrt(P)
BIG = 1.5 * 2.0 ** 23
TWO_PI = 2.0 * np.pi
PI1 = 6.28125
PI2 = float(np.float32(np.round((TWO_PI - PI1) * 2 ** 20) / 2 ** 20))
PI3 = float(TWO_PI - PI1 - PI2)
PI_MAX = 3.1415925

NORMS = [(0, "heads"), (0, "y"), (1, "heads"), (1, "y"), (2, "heads"), (2, "y"), (3, "heads"), (0, "x3"),
         (3, "y"), (1, "x3"), (2, "x3"), (3, "x3")]

TURNS = [(0, "y"), (1, "y"), (2, "y"), (0, "x3"), (3, "y"), (1, "x3"), (2, "x3"), (3, "x3")]

ROW_BQ, ROW_BK, ROW_BV, ROW_LNB, ROW_SW, ROW_LNS, ROW_MASK, ROW_TIME = 0, 16, 32, 48, 64, 80, 96, 112
C_ID, C_FOLD, C_TRI, C_DIV, C_OFF, C_IOTA, C_END = 0, 128, 256, 384, 512, 640, 657


def shape_constants():
    c = np.zeros((P, C_END), np.float32)
    c[:, C_ID:C_ID + P] = np.eye(P)
    fold = np.eye(P)
    fold[0, 1:] = -1.0
    fold[:, 0] = 0.0
    c[:, C_FOLD:C_FOLD + P] = fold
    c[:, C_TRI:C_TRI + P] = np.triu(np.ones((P, P)))
    i = np.arange(P)
    rate = (2.0 * (i // 2)).astype(np.float32) * np.float32(-np.log(10000.0) / P)
    c[:, C_DIV:C_DIV + P] = np.exp(rate)
    c[:, C_OFF:C_OFF + P] = 0.25 * (i % 2)
    c[:, C_IOTA:C_IOTA + E] = np.arange(E)
    c[:, C_IOTA + E] = np.arange(P)
    return c


def tower(nc, ids, times, mask, type_emb, Wq, bq, Wk, bk, Wv, bv, Wo, bo, ln_scale, ln_bias,
          final_scale, final_bias, switch_w, switch_b, expert_w, expert_b, const, out):
    with ExitStack() as ctx:
        def sb(name, shape, dt=F32):
            return ctx.enter_context(nc.sbuf_tensor(name, shape, dt))

        def sem(name):
            return ctx.enter_context(nc.semaphore(name))

        bank = [ctx.enter_context(nc.psum_tensor(f"bank{i}", [P, 512], F32)) for i in range(8)]
        SC = bank[0:2]
        SA = bank[2:4]
        TB = bank[4]
        XB = bank[5]
        OB = [t[:, 0:258].rearrange("p (c d) -> p c d", c=2) for t in bank[6:8]]
        EMB = [bank[i] for i in (1, 2, 3, 7)]
        LOGIT = TB[:, 0:NC * E].rearrange("p (c e) -> p c e", e=E)
        CUM = TB[:, 0:NC * E].rearrange("p (c e) -> p c e", e=E)

        K = sb("K", [P, C_END])
        ident = K[:, C_ID:C_ID + P]
        negident = sb("negident", [P, P], BF16)
        tri = sb("tri", [P, P], BF16)
        ones = sb("ones", [P, P], BF16)
        rows = sb("rows", [P, P])
        cols = sb("cols", [P, P])
        mask_i = sb("mask_i", [P, P], I32)
        mask_b = sb("mask_b", [P, B * S], I32)
        key_mask = sb("key_mask", [P, B, S])
        masked_all = sb("masked_all", [P, B])
        some_key = sb("some_key", [P, B])
        key_bias = sb("key_bias", [P, NT])
        fin_s = sb("fin_s", [P, P])
        fin_b = sb("fin_b", [P, P])
        sw_b = sb("sw_b", [P, 1])
        eb_rows = sb("eb_rows", [P, P])
        eb_cols = sb("eb_cols", [P, E])
        half = sb("half", [P, NC])
        eps_in = sb("eps_in", [P, NC])
        eps_sum = sb("eps_sum", [P, NC])
        ids_b = sb("ids_b", [V, B * S], I32)
        onehot = sb("onehot", [V, B * S])
        emb = sb("emb", [V, P])
        phase = sb("phase", [P, S])
        turns = sb("turns", [P, S])
        wave = sb("wave", [P, B, S])
        X = sb("X", [P, H, B, S])
        w_raw = sb("w_raw", [P, 4, P])
        bo_row = sb("bo_row", [1, P])
        fold_t = sb("fold_t", [P, P])
        lncol = sb("lncol", [P, 2])
        bias3 = sb("bias3", [P, 3])
        w_til = sb("w_til", [P, 3, P])
        g_hi = sb("g_hi", [P, P], F32R)
        g_lo = sb("g_lo", [P, P], F32R)
        wvo = sb("wvo", [P, P])
        stats = sb("stats", [P, NC, 6])
        mv = [sb(f"mv{i}", [P, NC, 2]) for i in range(2)]
        veps = [sb(f"veps{i}", [P, NC]) for i in range(2)]
        rstd = [sb(f"rstd{i}", [P, NC]) for i in range(2)]
        z = [sb(f"z{i}", [P, NC, P]) for i in range(2)]
        zT = [sb(f"zT{i}", [P, S]) for i in range(4)]
        zh = [sb(f"zh{i}", [P, S], F32R) for i in range(4)]
        zl = [sb(f"zl{i}", [P, S], F32R) for i in range(4)]
        th = [sb(f"th{i}", [P, S], F32R) for i in range(2)]
        tl = [sb(f"tl{i}", [P, S], F32R) for i in range(2)]
        val = [sb(f"val{i}", [P, NC, P + 1]) for i in range(4)]
        mcol = sb("mcol", [P, NC], BF16)
        prob = [sb(f"prob{i}", [P, S]) for i in range(NC)]
        rsum = sb("rsum", [P, NC])
        h0 = sb("h0", [P, B, S])
        h1 = sb("h1", [P, NT, P])
        x3 = sb("x3", [P, NT, P])
        x3_0 = sb("x3_0", [P, NT])
        square = sb("square", [P, B, NC, P], BF16)
        negsq = sb("negsq", [P, NC])
        logit = sb("logit", [P, NT, E])
        lexp = sb("lexp", [P, NT, E])
        top8 = sb("top8", [P, NT, 8])
        idx8 = sb("idx8", [P, NT, 8], U32)
        route1 = sb("route1", [P, NT, E], BF16)
        lsum = sb("lsum", [P, NT])
        rprob = sb("rprob", [P, NT])
        gate = sb("gate", [P, NT, E])
        group = sb("group", [P, NT, 4])
        member = sb("member", [P, NT, 4])
        drop = sb("drop", [P, NT])
        ew = sb("ew", [P, E, P])
        eh = sb("eh", [P, E, P], F32R)
        el = sb("el", [P, E, P], F32R)
        xg = [sb(f"xg{i}", [P, 4, P]) for i in range(2)]
        acc = [sb(f"acc{i}", [P, P]) for i in range(2)]
        acc_out = [sb(f"acc_out{i}", [P, P]) for i in range(2)]

        ld_const, ld_rows, ld_mask, ld_tail, ld_w = map(sem, "ld_const ld_rows ld_mask ld_tail ld_w".split())
        stored = [sem("stored_even"), sem("stored_odd")]
        rows_ready, cols_t, cols_ready, eb_t, eb_ready = map(sem, "rows_ready cols_t cols_ready eb_t eb_ready".split())
        onehot_ready, emb_ready, angle_ready, wave_ready = map(sem, "onehot_ready emb_ready angle_ready wave_ready".split())
        x_ready, x_copied, mask_ready, setup = map(sem, "x_ready x_copied mask_ready setup".split())
        lncol_ready, fold_ready, w1_ready, w1_copied = map(sem, "lncol_ready fold_ready w1_ready w1_copied".split())
        bias3_ready, w_til_ready, w2_ready, w2_copied, w_ready = map(
            sem, "bias3_ready w_til_ready w2_ready w2_copied w_ready".split())
        stats_ready, mv_ready, veps_ready, rstd_ready, z_ready = map(
            sem, "stats_ready mv_ready veps_ready rstd_ready z_ready".split())
        zt_ready, zt_copied, zhi_ready, zlo_ready = map(sem, "zt_ready zt_copied zhi_ready zlo_ready".split())
        v_ready, v_copied, t_ready, th_ready = map(sem, "v_ready v_copied t_ready th_ready".split())
        sa_ready, max_ready, inj_ready, row_ready, tl_ready = map(
            sem, "sa_ready max_ready inj_ready row_ready tl_ready".split())
        sc_ready, exp_done, av_done, rsum_ready, x_updated = map(
            sem, "sc_ready exp_done av_done rsum_ready x_updated".split())
        ew_sub, ew_folded, ew_turned, ew_high, ew_ready = map(sem, "ew_sub ew_folded ew_turned ew_high ew_ready".split())
        summed, y_ready, turned, turned_copied = map(sem, "summed y_ready turned turned_copied".split())
        tail_sc, tail_exp, tail_av, h1_ready, x3_ready = map(sem, "tail_sc tail_exp tail_av h1_ready x3_ready".split())
        logit_ready, lshift_ready, lexp_ready, routed, cum_ready, group_ready = map(
            sem, "logit_ready lshift_ready lexp_ready routed cum_ready group_ready".split())
        xg_ready, grouped, grouped_high, grouped_ready, expert_out, acc_ready = map(
            sem, "xg_ready grouped grouped_high grouped_ready expert_out acc_ready".split())
        chain = sem("chain")
        passed = sem("passed")

        def unit(g, j, ahead):
            gg, b = g + (j + ahead) // B, (j + ahead) % B
            if isinstance(gg, int) and not 0 <= gg < NG:
                return None
            return gg, b, gg * B + b

        def next_pair(g):
            return None if isinstance(g, int) and g + 1 >= NG else g + 1

        def last_pair(g):
            return isinstance(g, int) and g == NG - 1

        def at_least(eng, s, n):
            if not isinstance(n, int) or n > 0:
                eng.wait_ge(s, n)

        def apart(eng, s, n):
            at_least(eng, s, n)
            if not isinstance(n, int):
                eng.sem_inc(passed, 1)

        def run_steps(step):
            def run(eng):
                for g in (-1, 0):
                    for j in range(B):
                        step(g, j)
                with eng.Fori(1, NG - 1) as g:
                    for j in range(B):
                        step(g, j)
                for j in range(B):
                    step(NG - 1, j)
                step(NG, 0)
            return run

        block = ctx.enter_context(nc.Block())

        @block.sync
        def _(sp):
            sp.dma_start(rows[ROW_TIME:ROW_TIME + NT, :],
                         times.rearrange("b (c p) -> (b c) p", p=P)).then_inc(ld_rows, 16)
            sp.dma_start(mask_i[ROW_MASK:ROW_MASK + NT, :],
                         mask.rearrange("b (c p) -> (b c) p", p=P)).then_inc(ld_rows, 16)
            sp.dma_start(rows[ROW_SW:ROW_SW + E, :], switch_w).then_inc(ld_rows, 16)
            sp.dma_start(sw_b[ROW_SW:ROW_SW + E, :], switch_b.rearrange("(e a) -> e a", a=1)).then_inc(ld_rows, 16)
            for a, at in ((bq, ROW_BQ), (bk, ROW_BK), (bv, ROW_BV), (ln_bias, ROW_LNB), (ln_scale, ROW_LNS)):
                for l in range(L):
                    sp.dma_start(rows[at + l * H:at + (l + 1) * H, :], a[:, l, :]).then_inc(ld_rows, 16)

            def step(g, j):
                gw = next_pair(g)
                if j == 0 and gw is not None:
                    at_least(sp, w_ready, gw)
                    i = (gw % H) * L + gw // H
                    for k, w in enumerate((Wq, Wk, Wv, Wo)):
                        v = w.rearrange("h l a b -> (h l) a b")
                        sp.dma_start(w_raw[:, k, :], v[bass.ds(i, 1), :, :].rearrange("o a b -> a (o b)")).then_inc(ld_w, 16)
                    sp.dma_start(bo_row[:, :], bo.rearrange("h l d -> (h l) d")[bass.ds(i, 1), :]).then_inc(ld_w, 16)
                if isinstance(g, int) and g == -1 and j == 0:
                    sp.dma_start(mask_b[:, :], mask.rearrange("b s -> (b s)").unsqueeze(0).to_broadcast([P, B * S])).then_inc(ld_mask, 16)
                    sp.dma_start(ew[:, :, :], expert_w.rearrange("e f d -> f e d")).then_inc(ld_tail, 16)
                    sp.dma_start(eb_rows[0:E, :], expert_b).then_inc(ld_tail, 16)
                    sp.dma_start(fin_s[:, :], final_scale.unsqueeze(0).to_broadcast([P, P])).then_inc(ld_tail, 16)
                    sp.dma_start(fin_b[:, :], final_bias.unsqueeze(0).to_broadcast([P, P])).then_inc(ld_tail, 16)

            run_steps(step)(sp)
            for j in range(NT):
                sp.wait_ge(acc_ready, j + 1)
                sp.dma_start(out.rearrange("b (c p) d -> (b c) p d", p=P)[j], acc_out[j % 2][:, :]).then_inc(stored[j % 2], 16)
            for s in stored:
                sp.wait_ge(s, 16 * NT // 2)

        @block.tensor
        def _(pe):
            pe.wait_ge(onehot_ready, 1)
            for b in range(B):
                for c in range(NC):
                    mm = pe.matmul(EMB[b][:, c * P:(c + 1) * P],
                                   onehot[:, (b * NC + c) * P:(b * NC + c + 1) * P], emb[:, :],
                                   start=True, stop=True)
                mm.then_inc(emb_ready, 1)
            pe.wait_ge(rows_ready, 2)
            pe.transpose(bank[0][:, 0:P], rows[:, :], ident).then_inc(cols_t, 1)
            pe.wait_ge(ld_tail, 64)
            pe.transpose(TB[:, 0:E], eb_rows[0:E, :], K[0:E, C_ID:C_ID + E]).then_inc(eb_t, 1)

            def scores(u, kc):
                g, b, n = u
                at_least(pe, exp_done, NC * n + kc - 1)
                if kc == 0:
                    at_least(pe, tl_ready, n + 1)
                    if isinstance(g, int) and n == 0:
                        pe.wait_ge(x_ready, B)
                ks = slice(kc * P, (kc + 1) * P)
                o = SC[kc % 2][:, :]
                pe.matmul(o, zh[b][:, ks], th[b % 2][:, :], start=True, stop=False)
                pe.matmul(o, zh[b][:, ks], tl[b % 2][:, :], start=False, stop=False)
                pe.matmul(o, zl[b][:, ks], th[b % 2][:, :], start=False, stop=True).then_inc(sc_ready, 1)

            def times_values(u, kc):
                g, b, n = u
                at_least(pe, exp_done, NC * n + kc + 1)
                if kc == 0:
                    at_least(pe, x_updated, n)
                for c in range(NC):
                    mm = pe.matmul(OB[c // 2][:, c % 2, :], prob[kc][:, c * P:(c + 1) * P],
                                   val[b][:, kc, :], start=(kc == 0 and c % 2 == 0), stop=(kc == NC - 1),
                                   skip_group_check=True)
                mm.then_inc(av_done, 1)

            def rough_scores(u, c):
                g, b, n = u
                if c == 0:
                    at_least(pe, th_ready, n + 1)
                    if isinstance(g, int) and n == 0:
                        pe.wait_ge(x_ready, 3)
                at_least(pe, max_ready, NC * n + c - 1)
                pe.matmul(SA[c % 2][:, :], th[b % 2][:, c * P:(c + 1) * P], zh[b][:, :],
                          start=True, stop=True).then_inc(sa_ready, 1)

            def turn_z(u):
                g, b, n = u
                at_least(pe, z_ready, n + 1)
                at_least(pe, v_copied, n)
                for c in range(NC):
                    mm = pe.transpose(XB[:, c * P:(c + 1) * P], z[b % 2][:, c, :], ident)
                mm.then_inc(zt_ready, 1)

            def values(u):
                g, b, n = u
                at_least(pe, zt_copied, n + 1)
                at_least(pe, w_ready, g + 1)
                for c in range(NC):
                    mm = pe.matmul(XB[:, c * P:(c + 1) * P], zT[b][:, c * P:(c + 1) * P], wvo[:, :],
                                   start=True, stop=True)
                mm.then_inc(v_ready, 1)

            def project(u):
                g, b, n = u
                at_least(pe, zlo_ready, n + 1)
                at_least(pe, tl_ready, n)
                pe.matmul(TB[:, :], g_hi[:, :], zh[b][:, :], start=True, stop=False)
                pe.matmul(TB[:, :], g_hi[:, :], zl[b][:, :], start=False, stop=False)
                pe.matmul(TB[:, :], g_lo[:, :], zh[b][:, :], start=False, stop=True).then_inc(t_ready, 1)

            def inject(u):
                g, b, n = u
                at_least(pe, max_ready, NC * (n + 1))
                for c in range(NC):
                    mm = pe.matmul(TB[0:1, c * P:(c + 1) * P], mcol[:, c:c + 1], negident[:, :],
                                   start=False, stop=True, skip_group_check=True)
                mm.then_inc(inj_ready, 1)

            def fold_1(gw, n2):
                at_least(pe, fold_ready, gw + 1)
                at_least(pe, ld_w, 80 * (gw + 1))
                if n2:
                    at_least(pe, zt_copied, n2[2] + 1)
                for k in range(3):
                    mm = pe.matmul(XB[:, k * P:(k + 1) * P], w_raw[:, k, :], fold_t[:, :], start=True, stop=True)
                mm.then_inc(w1_ready, 1)

            def fold_2(gw):
                at_least(pe, w_til_ready, gw + 1)
                at_least(pe, v_copied, gw * B - 1)
                pe.matmul(XB[:, 0:P], w_til[:, 0, :], w_til[:, 1, :], start=True, stop=True)
                pe.matmul(XB[:, P:2 * P], w_til[:, 2, :], w_raw[:, 3, :], start=True, stop=True).then_inc(w2_ready, 1)

            def turn_experts(q):
                pe.wait_ge(ew_folded, 4)
                if q:
                    pe.wait_ge(ew_ready, q)
                for k in range(4):
                    mm = pe.transpose(XB[:, k * P:(k + 1) * P], ew[:, 4 * q + k, :], ident)
                mm.then_inc(ew_turned, 1)

            def step(g, j):
                last, now, nxt, nxt2 = (unit(g, j, a) for a in (-1, 0, 1, 2))
                gw = next_pair(g)
                if now: scores(now, 0)
                if j == 2 and gw is not None: fold_2(gw)
                if last: times_values(last, 2)
                if nxt: rough_scores(nxt, 0)
                if j == 2 and gw is not None:
                    at_least(pe, w_ready, gw + 1)
                if last_pair(g) and j >= 2: turn_experts(2 * j - 4)
                if nxt2: turn_z(nxt2)
                if nxt: rough_scores(nxt, 1)
                if last: times_values(last, 3)
                if now: scores(now, 1)
                if nxt: rough_scores(nxt, 2)
                if j == 1 and gw is not None:
                    at_least(pe, v_copied, gw * B - 1)
                    fold_1(gw, nxt2)
                if nxt: rough_scores(nxt, 3)
                if now: scores(now, 2)
                if nxt2:
                    if j == 1 and gw is not None:
                        at_least(pe, w1_copied, g + 2)
                    values(nxt2)
                if last_pair(g) and j >= 2: turn_experts(2 * j - 3)
                if nxt: inject(nxt)
                if now: times_values(now, 0)
                if now: scores(now, 3)
                if now: times_values(now, 1)
                if nxt2: project(nxt2)

            run_steps(step)(pe)

            def turn_rows(b, what):
                i = TURNS.index((b, what))
                if i == 0:
                    pe.wait_ge(ew_ready, 4)
                pe.wait_ge(*((y_ready, b + 1) if what == "y" else (x3_ready, b + 1)))
                if i:
                    pe.wait_ge(turned_copied, i)
                for c in range(NC):
                    mm = pe.transpose(XB[:, c * P:(c + 1) * P], val[b][:, c, 0:P] if what == "y" else x3[:, b * NC + c, :], ident)
                mm.then_inc(turned, 1)

            def tail_values(b, kc):
                pe.wait_ge(tail_exp, NC * b + kc + 1)
                if kc == 0:
                    pe.wait_ge(*((h1_ready, b) if b else (x_updated, NU)))
                for c in range(NC):
                    mm = pe.matmul(OB[c // 2][:, c % 2, :], prob[kc][:, c * P:(c + 1) * P], val[b][:, kc, :],
                                   start=(kc == 0 and c % 2 == 0), stop=(kc == NC - 1), skip_group_check=True)
                mm.then_inc(tail_av, 1)

            def tail_scores(b, kc):
                if kc == 0:
                    pe.wait_ge(turned_copied, TURNS.index((b, "y")) + 1)
                if NC * b + kc >= 2:
                    pe.wait_ge(tail_exp, NC * b + kc - 1)
                pe.matmul(SC[kc % 2][:, :], ones[:, :], square[:, b, :, :], start=True, stop=False)
                pe.matmul(SC[kc % 2][:, :], zT[b][:, kc * P:(kc + 1) * P], zT[b][:, :],
                          start=False, stop=True).then_inc(tail_sc, 1)

            def attend(b):
                tail_scores(b, 0)
                tail_scores(b, 1)
                if b == 2: logits(0)
                tail_values(b, 0)
                tail_scores(b, 2)
                tail_values(b, 1)
                tail_scores(b, 3)
                if b < B - 1: turn_rows(b + 1, "y")
                if b == 3: logits(1)
                tail_values(b, 2)
                tail_values(b, 3)

            def logits(b):
                pe.wait_ge(turned_copied, TURNS.index((b, "x3")) + 1)
                if b:
                    pe.wait_ge(group_ready, b)
                for c in range(NC):
                    mm = pe.matmul(LOGIT[:, c, :], zT[b][:, c * P:(c + 1) * P], cols[:, ROW_SW:ROW_SW + E],
                                   start=True, stop=True)
                mm.then_inc(logit_ready, 1)

            def count_routes(b):
                pe.wait_ge(routed, b + 1)
                pe.matmul(CUM, tri[:, :], route1[:, b * NC:(b + 1) * NC, :], start=True, stop=True)
                for i in range((b + 1) * NC - 1):
                    c = max(i + 1 - b * NC, 0)
                    mm = pe.matmul(CUM[:, c:NC, :], ones[:, :], route1[:, i:i + 1, :].to_broadcast([P, NC - c, E]),
                                   start=False, stop=True, skip_group_check=True)
                mm.then_inc(cum_ready, 1)

            def turn_groups(j):
                if j < NT:
                    pe.wait_ge(xg_ready, j + 1)
                    if j >= 2:
                        pe.wait_ge(grouped_ready, j - 1)
                    for a in range(4):
                        mm = pe.transpose(SA[j % 2][:, a * P:(a + 1) * P], xg[j % 2][:, a, :], ident)
                    mm.then_inc(grouped, 1)

            def experts(j):
                pe.wait_ge(grouped_ready, j + 1)
                if j < 2:
                    pe.wait_ge(tail_exp, NC * B)
                else:
                    pe.wait_ge(acc_ready, j - 1)
                o = SC[j % 2][:, :]
                for a in range(4):
                    js, es = slice(a * P, (a + 1) * P), slice(4 * a, 4 * a + 4)
                    pe.matmul(o, th[j % 2][:, js], eh[:, es, :], start=(a == 0), stop=False)
                    pe.matmul(o, th[j % 2][:, js], el[:, es, :], start=False, stop=False)
                    mm = pe.matmul(o, tl[j % 2][:, js], eh[:, es, :], start=False, stop=(a == 3))
                mm.then_inc(expert_out, 1)

            turn_rows(0, "y")
            attend(0)
            attend(1)
            turn_rows(0, "x3")
            attend(2)
            turn_rows(1, "x3")
            count_routes(0)
            attend(3)
            turn_rows(2, "x3")
            count_routes(1)
            turn_groups(0)
            for j in range(NT):
                turn_groups(j + 1)
                experts(j)
                if j == 1: logits(2)
                if j == 3:
                    turn_rows(3, "x3")
                    count_routes(2)
                if j == 5: logits(3)
                if j == 6: count_routes(3)

        @block.scalar
        def _(act):
            act.dma_start(K[:, :], const).then_inc(ld_const, 16)
            act.dma_start(ids_b[:, :], ids.rearrange("b s -> (b s)").unsqueeze(0).to_broadcast([V, B * S])).then_inc(ld_const, 16)
            act.dma_start(emb[:, :], type_emb).then_inc(ld_const, 16)
            act.wait_ge(cols_t, 1)
            act.copy(cols[:, :], bank[0][:, 0:P]).then_inc(cols_ready, 1)
            act.wait_ge(eb_t, 1)
            act.copy(eb_cols[:, :], TB[:, 0:E]).then_inc(eb_ready, 1)
            for b in range(B):
                act.wait_ge(angle_ready, b + 1)
                act.activation(wave[:, b, :], wave[:, b, :], ACT.Sin).then_inc(wave_ready, 1)

            def exps(u, kc):
                g, b, n = u
                at_least(act, sc_ready, NC * n + kc + 1)
                at_least(act, av_done, NC * (n - 1) + kc + 1)
                act.activation(prob[kc][:, :], SC[kc % 2][:, :], ACT.Exp,
                               bias=key_bias[:, b * NC + kc:b * NC + kc + 1]).then_inc(exp_done, 1)

            def step(g, j):
                now, nxt, nxt2 = (unit(g, j, a) for a in (0, 1, 2))
                gw = next_pair(g)
                if now: exps(now, 0)
                if j == 2 and gw is not None:
                    at_least(act, w2_ready, gw + 1)
                    act.activation(g_hi[:, :], XB[:, 0:P], ACT.Identity, scale=float(SCALE)).then_inc(w2_copied, 1)
                    act.copy(wvo[:, :], XB[:, P:2 * P]).then_inc(w2_copied, 1)
                if last_pair(g) and j >= 2: experts_high(2 * j - 4)
                if nxt2:
                    at_least(act, zt_ready, nxt2[2] + 1)
                    act.copy(zh[nxt2[1]][:, :], XB[:, :]).then_inc(zhi_ready, 1)
                    act.copy(zT[nxt2[1]][:, :], XB[:, :]).then_inc(zt_copied, 1)
                if now: exps(now, 1)
                if j == 1 and gw is not None:
                    at_least(act, w1_ready, gw + 1)
                    act.copy(w_til[:, :, :], XB[:, 0:3 * P].rearrange("p (k d) -> p k d", k=3)).then_inc(w1_copied, 1)
                if now: exps(now, 2)
                if last_pair(g) and j >= 2: experts_high(2 * j - 3)
                if nxt2:
                    at_least(act, v_ready, nxt2[2] + 1)
                    act.copy(val[nxt2[1]][:, :, 0:P], XB[:, :].rearrange("p (c d) -> p c d", c=NC)).then_inc(v_copied, 1)
                if nxt:
                    at_least(act, inj_ready, nxt[2] + 1)
                    act.activation(th[nxt[1] % 2][0:1, :], TB[0:1, :], ACT.Identity,
                                   scale=some_key[0:1, nxt[1]:nxt[1] + 1]).then_inc(row_ready, 1)
                if now: exps(now, 3)
                if nxt2:
                    at_least(act, t_ready, nxt2[2] + 1)
                    act.activation(th[nxt2[1] % 2][:, :], TB[:, :], ACT.Identity,
                                   scale=some_key[:, nxt2[1]:nxt2[1] + 1]).then_inc(th_ready, 1)

            def experts_high(q):
                act.wait_ge(ew_turned, q + 1)
                act.copy(eh[:, 4 * q:4 * q + 4, :], XB[:, :].rearrange("p (k d) -> p k d", k=4)).then_inc(ew_high, 1)

            act.wait_ge(mask_ready, 1)
            run_steps(step)(act)

            def turned_copy(b, i):
                act.wait_ge(turned, i + 1)
                act.copy(zT[b][:, :], XB[:, :]).then_inc(turned_copied, 1)

            def attention_exps(b):
                for kc in range(NC):
                    act.wait_ge(tail_sc, NC * b + kc + 1)
                    if b:
                        act.wait_ge(tail_av, NC * (b - 1) + kc + 1)
                    act.activation(prob[kc][:, :], SC[kc % 2][:, :], ACT.Exp).then_inc(tail_exp, 1)
                    if kc == 2 and b < B - 1:
                        turned_copy(b + 1, TURNS.index((b + 1, "y")))

            def route_exps(b):
                js = slice(b * NC, (b + 1) * NC)
                act.wait_ge(lshift_ready, b + 1)
                act.activation(lexp[:, js, :], lexp[:, js, :], ACT.Exp).then_inc(lexp_ready, 1)

            def group_rows(j):
                if j < NT:
                    act.wait_ge(group_ready, j // NC + 1)
                    for a in range(4):
                        ins = act.activation(xg[j % 2][:, a, :], x3[:, j, :], ACT.Identity, scale=group[:, j, a:a + 1])
                    ins.then_inc(xg_ready, 1)

            turned_copy(0, 0)
            attention_exps(0)
            attention_exps(1)
            turned_copy(0, TURNS.index((0, "x3")))
            attention_exps(2)
            route_exps(0)
            turned_copy(1, TURNS.index((1, "x3")))
            attention_exps(3)
            route_exps(1)
            turned_copy(2, TURNS.index((2, "x3")))
            group_rows(0)
            group_rows(1)
            for j in range(NT):
                act.wait_ge(grouped, j + 1)
                if j >= 2:
                    act.wait_ge(expert_out, j - 1)
                act.copy(th[j % 2][:, :], SA[j % 2][:, :]).then_inc(grouped_high, 1)
                group_rows(j + 2)
                if j == 2: route_exps(2)
                if j == 4: turned_copy(3, TURNS.index((3, "x3")))
                if j == 6: route_exps(3)

        @block.vector
        def _(dve):
            count = [0]

            def then(ins):
                count[0] += 1
                ins.then_inc(chain, 1)
                dve.wait_ge(chain, count[0])

            for t in z + [x3]:
                dve.memset(t[:, :, 0:1], 1.0)
            for t in val:
                dve.memset(t[:, :, P:P + 1], 1.0)
            dve.memset(half[:, :], -0.5)
            dve.memset(eps_in[:, :], EPS)
            dve.memset(eps_sum[:, :], H * H * EPS)
            dve.memset(ones[:, :], 1.0)
            dve.wait_ge(ld_const, 48)
            dve.tensor_scalar(onehot[:, :], ids_b[:, :], K[0:V, C_IOTA + E:C_IOTA + E + 1], None,
                              ALU.is_equal).then_inc(onehot_ready, 1)
            dve.wait_ge(ld_rows, 16 * 24)
            sw_rows = rows[ROW_SW:ROW_SW + E, :]
            then(dve.tensor_scalar(sw_rows[:, 1:P], sw_rows[:, 1:P], sw_rows[:, 0:1], None, ALU.subtract))
            dve.tensor_copy(sw_rows[:, 0:1], sw_b[ROW_SW:ROW_SW + E, :]).then_inc(rows_ready, 1)
            dve.tensor_scalar(rows[ROW_MASK:ROW_MASK + NT, :], mask_i[ROW_MASK:ROW_MASK + NT, :], 0, NEG,
                              ALU.is_equal, ALU.mult).then_inc(rows_ready, 1)
            dve.tensor_copy(tri[:, :], K[:, C_TRI:C_TRI + P])
            dve.tensor_scalar(negident[:, :], ident, -1.0, None, ALU.mult).then_inc(setup, 1)

            def encode(b):
                tcol = cols[:, ROW_TIME + b * NC:ROW_TIME + (b + 1) * NC]
                ph = phase[:, :].rearrange("p (c d) -> p c d", c=NC)
                div = K[:, C_DIV:C_DIV + P].unsqueeze(1).to_broadcast([P, NC, P])
                off = K[:, C_OFF:C_OFF + P].unsqueeze(1).to_broadcast([P, NC, P])
                tu = turns[:, :].rearrange("p (c d) -> p c d", c=NC)
                an = wave[:, b, :].rearrange("p (c d) -> p c d", c=NC)
                then(dve.tensor_tensor(ph, tcol.unsqueeze(2).to_broadcast([P, NC, P]), div, ALU.mult))
                then(dve.scalar_tensor_tensor(out=tu, in0=ph, scalar=float(1.0 / TWO_PI), in1=off, op0=ALU.mult, op1=ALU.add))
                then(dve.tensor_scalar(turns[:, :], turns[:, :], BIG, BIG, ALU.add, ALU.subtract))
                then(dve.scalar_tensor_tensor(out=ph, in0=tu, scalar=-PI1, in1=ph, op0=ALU.mult, op1=ALU.add))
                then(dve.scalar_tensor_tensor(out=ph, in0=tu, scalar=-PI2, in1=ph, op0=ALU.mult, op1=ALU.add))
                then(dve.scalar_tensor_tensor(out=ph, in0=tu, scalar=-PI3, in1=ph, op0=ALU.mult, op1=ALU.add))
                then(dve.scalar_tensor_tensor(out=an, in0=off, scalar=TWO_PI, in1=ph, op0=ALU.mult, op1=ALU.add))
                dve.tensor_scalar(wave[:, b, :], wave[:, b, :], PI_MAX, -PI_MAX, ALU.min, ALU.max).then_inc(angle_ready, 1)

            dve.wait_ge(cols_ready, 1)
            for b in range(B):
                encode(b)
            dve.wait_ge(ld_mask, 16)
            then(dve.tensor_scalar(key_mask[:, :, :].rearrange("p b s -> p (b s)"), mask_b[:, :], 0, NEG, ALU.is_equal, ALU.mult))
            then(dve.tensor_reduce(masked_all[:, :], key_mask[:, :, :], AX.X, ALU.max))
            then(dve.tensor_scalar(some_key[:, :], masked_all[:, :], 0.0, None, ALU.is_equal))
            for b in range(B):
                dve.tensor_scalar(key_mask[:, b, :], key_mask[:, b, :], some_key[:, b:b + 1], None, ALU.mult)
            dve.tensor_tensor(key_bias[:, :].rearrange("p (b c) -> p b c", b=B),
                              cols[:, ROW_MASK:ROW_MASK + NT].rearrange("p (b c) -> p b c", b=B),
                              some_key[:, :].unsqueeze(2).to_broadcast([P, B, NC]), ALU.mult).then_inc(mask_ready, 1)
            dve.wait_ge(mask_ready, 1)

            def maxima(u, c):
                g, b, n = u
                if c == 0:
                    apart(dve, inj_ready, n)
                apart(dve, sa_ready, NC * n + c + 1)
                sa = SA[c % 2][:, :]
                dve.tensor_tensor_reduce(out=sa, in0=sa, in1=key_mask[:, b, :], scale=1.0, scalar=-3e38,
                                         op0=ALU.add, op1=ALU.max, accum_out=mcol[:, c:c + 1]).then_inc(max_ready, 1)

            def row_stats(x, n, i):
                for c in range(NC):
                    ins = dve.bn_stats(stats[:, c, :], x[:, c * P:(c + 1) * P])
                ins.then_inc(stats_ready, 1)
                apart(dve, rstd_ready, n - 1)
                apart(dve, stats_ready, n + 1)
                for c in range(NC):
                    ins = dve.bn_aggr(mv[i][:, c, :], stats[:, c, :])
                ins.then_inc(mv_ready, 1)

            def step(g, j):
                last, now, nxt, nxt2, nxt3 = (unit(g, j, a) for a in (-1, 0, 1, 2, 3))
                gw = next_pair(g)
                if nxt3 and nxt3[2] is not None and isinstance(nxt3[0], int) and nxt3[0] == 0:
                    b = nxt3[1]
                    dve.wait_ge(wave_ready, b + 1)
                    dve.wait_ge(emb_ready, b + 1)
                    dve.tensor_tensor(X[:, 0, b, :], wave[:, b, :], EMB[b][:, :], ALU.add).then_inc(x_ready, 1)
                    dve.wait_ge(x_ready, b + 1)
                if isinstance(g, int) and g == 0 and j:
                    dve.wait_ge(x_copied, B if j == 3 else j)
                if j == 2 and gw is not None:
                    at_least(dve, w2_copied, 2 * (gw + 1))
                    dve.scalar_tensor_tensor(out=g_lo[:, :], in0=XB[:, 0:P], scalar=float(SCALE), in1=g_hi[:, :].bitcast(F32),
                                             op0=ALU.mult, op1=ALU.subtract)
                    dve.tensor_tensor(wvo[0:1, :], wvo[0:1, :], bo_row[:, :], ALU.add).then_inc(w_ready, 1)
                if nxt: maxima(nxt, 0)
                if last_pair(g) and j >= 2: experts_low(2 * j - 4)
                if nxt: maxima(nxt, 1)
                if last:
                    g_, b_, n_ = last
                    at_least(dve, av_done, NC * (n_ + 1))
                    dve.reciprocal(rsum[:, 0:2], OB[0][:, :, P])
                    dve.reciprocal(rsum[:, 2:4], OB[1][:, :, P]).then_inc(rsum_ready, 1)
                    at_least(dve, rsum_ready, n_ + 1)
                    if last_pair(g_):
                        dve.wait_ge(summed, (H - 1) * (b_ + 1))
                    for c in range(NC):
                        xs = h0[:, b_, c * P:(c + 1) * P] if last_pair(g_) else X[:, g_ % H, b_, c * P:(c + 1) * P]
                        ins = dve.scalar_tensor_tensor(out=xs, in0=OB[c // 2][:, c % 2, 0:P], scalar=rsum[:, c:c + 1],
                                                       in1=xs, op0=ALU.mult, op1=ALU.add)
                    ins.then_inc(x_updated, 1)
                if nxt: maxima(nxt, 2)
                if nxt: maxima(nxt, 3)
                if last_pair(g) and j >= 2: experts_low(2 * j - 3)
                if nxt2:
                    at_least(dve, zt_copied, nxt2[2] + 1)
                    dve.tensor_tensor(zl[nxt2[1]][:, :], zT[nxt2[1]][:, :], zh[nxt2[1]][:, :].bitcast(F32),
                                      ALU.subtract).then_inc(zlo_ready, 1)
                if nxt3:
                    row_stats(X[:, nxt3[0] % H, nxt3[1], :], nxt3[2], nxt3[1] % 2)
                if nxt:
                    at_least(dve, row_ready, nxt[2] + 1)
                    t = nxt[1] % 2
                    dve.scalar_tensor_tensor(out=tl[t][:, :], in0=TB[:, :], scalar=some_key[:, nxt[1]:nxt[1] + 1],
                                             in1=th[t][:, :].bitcast(F32), op0=ALU.mult, op1=ALU.subtract).then_inc(tl_ready, 1)
                if nxt3:
                    at_least(dve, rstd_ready, nxt3[2] + 1)
                    at_least(dve, zt_ready, nxt3[2] - 1)
                    for c in range(NC):
                        ins = dve.tensor_scalar(z[nxt3[1] % 2][:, c, 1:P], X[:, nxt3[0] % H, nxt3[1], c * P + 1:(c + 1) * P],
                                                mv[nxt3[1] % 2][:, c, 0:1], rstd[nxt3[1] % 2][:, c:c + 1],
                                                ALU.subtract, ALU.mult)
                    ins.then_inc(z_ready, 1)
                if last_pair(g) and j == 1:
                    heads_norm(0)
                if last_pair(g) and j == 2:
                    encoder_output(0)
                    attention_input(0)
                if last_pair(g) and j == 3:
                    heads_norm(1)
                    encoder_output(1)
                    attention_input(1)

            def experts_low(q):
                dve.wait_ge(ew_high, q + 1)
                dve.tensor_tensor(el[:, 4 * q:4 * q + 4, :], XB[:, :].rearrange("p (k d) -> p k d", k=4),
                                  eh[:, 4 * q:4 * q + 4, :].bitcast(F32), ALU.subtract).then_inc(ew_ready, 1)

            def stats_of(b, what, x):
                i = NORMS.index((b, what))
                row_stats(x, NU + i, i % 2)

            def factors(b, what):
                i = NORMS.index((b, what))
                dve.wait_ge(rstd_ready, NU + i + 1)
                return mv[i % 2][:, :, 0], mv[i % 2][:, :, 1], rstd[i % 2]

            def normalised(out_, x, mean, factor, c):
                return dve.tensor_scalar(out_, x, mean[:, c:c + 1], factor[:, c:c + 1], ALU.subtract, ALU.mult)

            def heads_norm(b):
                dve.wait_ge(x_updated, NU - B + b + 1)
                stats_of(b, "heads", h0[:, b, :])

            def encoder_output(b):
                h3 = h0[:, b, :].rearrange("p (c d) -> p c d", c=NC)
                dve.wait_ge(ld_tail, 64)
                mean, _, factor = factors(b, "heads")
                for c in range(NC):
                    ins = normalised(h3[:, c, :], h3[:, c, :], mean, factor, c)
                then(ins)
                then(dve.tensor_tensor(h3, h3, fin_s[:, :].unsqueeze(1).to_broadcast([P, NC, P]), ALU.mult))
                then(dve.tensor_tensor(h3, h3, fin_b[:, :].unsqueeze(1).to_broadcast([P, NC, P]), ALU.add))
                stats_of(b, "y", h0[:, b, :])

            def attention_input(b):
                h3 = h0[:, b, :].rearrange("p (c d) -> p c d", c=NC)
                mean, variance, factor = factors(b, "y")
                then(dve.tensor_tensor(negsq[:, :], variance, factor[:, :], ALU.mult))
                then(dve.scalar_tensor_tensor(out=negsq[:, :], in0=negsq[:, :], scalar=-float(P), in1=factor[:, :],
                                              op0=ALU.mult, op1=ALU.mult))
                for c in range(NC):
                    normalised(val[b][:, c, 0:P], h3[:, c, :], mean, factor, c)
                dve.tensor_tensor(square[:, b, :, :], ident.unsqueeze(1).to_broadcast([P, NC, P]),
                                  negsq[:, :].unsqueeze(2).to_broadcast([P, NC, P]), ALU.mult).then_inc(y_ready, 1)

            run_steps(step)(dve)

            def attended(b):
                dve.wait_ge(tail_av, NC * (b + 1))
                dve.reciprocal(rsum[:, 0:2], OB[0][:, :, P])
                then(dve.reciprocal(rsum[:, 2:4], OB[1][:, :, P]))
                for c in range(NC):
                    ins = dve.scalar_tensor_tensor(out=h1[:, b * NC + c, :], in0=OB[c // 2][:, c % 2, 0:P], scalar=rsum[:, c:c + 1],
                                                   in1=h0[:, b, c * P:(c + 1) * P], op0=ALU.mult, op1=ALU.add)
                ins.then_inc(h1_ready, 1)
                dve.wait_ge(h1_ready, b + 1)
                stats_of(b, "x3", h1[:, b * NC:(b + 1) * NC, :].rearrange("p c d -> p (c d)"))

            def experts_input(b):
                js = slice(b * NC, (b + 1) * NC)
                mean, _, factor = factors(b, "x3")
                for c in range(NC):
                    j = b * NC + c
                    normalised(x3[:, j, 1:P], h1[:, j, 1:P], mean, factor, c)
                then(dve.tensor_tensor(x3_0[:, js], h1[:, js, 0], mean, ALU.subtract))
                dve.tensor_tensor(x3_0[:, js], x3_0[:, js], factor[:, :], ALU.mult).then_inc(x3_ready, 1)

            def route(b):
                js = slice(b * NC, (b + 1) * NC)
                dve.wait_ge(logit_ready, b + 1)
                then(dve.tensor_copy(logit[:, js, :], LOGIT))
                for c in range(NC):
                    ins = dve.max(top8[:, b * NC + c, :], logit[:, b * NC + c, :])
                then(ins)
                dve.tensor_tensor(lexp[:, js, :], logit[:, js, :], top8[:, js, 0:1].to_broadcast([P, NC, E]),
                                  ALU.subtract).then_inc(lshift_ready, 1)
                for c in range(NC):
                    ins = dve.max_index(idx8[:, b * NC + c, :], top8[:, b * NC + c, :], logit[:, b * NC + c, :])
                then(ins)
                dve.tensor_tensor(route1[:, js, :], K[:, C_IOTA:C_IOTA + E].unsqueeze(1).to_broadcast([P, NC, E]),
                                  idx8[:, js, 0:1].to_broadcast([P, NC, E]), ALU.is_equal).then_inc(routed, 1)

            def choose(b):
                js = slice(b * NC, (b + 1) * NC)
                dve.wait_ge(lexp_ready, b + 1)
                dve.tensor_reduce(lsum[:, js], lexp[:, js, :], AX.X, ALU.add)
                dve.wait_ge(cum_ready, b + 1)
                then(dve.scalar_tensor_tensor(out=gate[:, js, :], in0=CUM, scalar=float(CAP) + 0.5, in1=route1[:, js, :],
                                              op0=ALU.is_le, op1=ALU.mult))
                dve.tensor_reduce(group[:, js, :], gate[:, js, :].rearrange("p c (a i) -> p c a i", i=4), AX.X,
                                  ALU.add).then_inc(group_ready, 1)
                dve.tensor_reduce(member[:, js, :], gate[:, js, :].rearrange("p c (a i) -> p c i a", i=4), AX.X, ALU.add)
                then(dve.reciprocal(rprob[:, js], lsum[:, js]))
                dve.wait_ge(group_ready, b + 1)
                dve.tensor_reduce(drop[:, js], group[:, js, :], AX.X, ALU.add)
                then(dve.tensor_tensor(member[:, js, :], member[:, js, :], rprob[:, js].unsqueeze(2).to_broadcast([P, NC, 4]),
                                       ALU.mult))
                then(dve.tensor_scalar(drop[:, js], drop[:, js], -1.0, 1.0, ALU.mult, ALU.add))
                then(dve.tensor_tensor(drop[:, js], drop[:, js], rprob[:, js], ALU.mult))
                then(dve.scalar_tensor_tensor(out=x3_0[:, js], in0=x3_0[:, js], scalar=-1.0, in1=drop[:, js],
                                              op0=ALU.add, op1=ALU.mult))
                then(dve.tensor_tensor(h1[:, js, 0], h1[:, js, 0], x3_0[:, js], ALU.add))

            def grouped_low(j):
                dve.wait_ge(grouped_high, j + 1)
                dve.tensor_tensor(tl[j % 2][:, :], SA[j % 2][:, :], th[j % 2][:, :].bitcast(F32),
                                  ALU.subtract).then_inc(grouped_ready, 1)

            def add_experts(j):
                a = acc[j % 2][:, :]
                then(dve.scalar_tensor_tensor(out=a, in0=x3[:, j, :], scalar=drop[:, j:j + 1], in1=h1[:, j, :],
                                              op0=ALU.mult, op1=ALU.add))
                dve.wait_ge(expert_out, j + 1)
                if j >= 2:
                    dve.wait_ge(stored[j % 2], 16 * (j // 2))
                for i in range(4):
                    ins = dve.scalar_tensor_tensor(out=a if i < 3 else acc_out[j % 2][:, :], in0=SC[j % 2][:, i * P:(i + 1) * P],
                                                   scalar=member[:, j, i:i + 1], in1=a, op0=ALU.mult, op1=ALU.add)
                    if i < 3:
                        then(ins)
                ins.then_inc(acc_ready, 1)

            heads_norm(2)
            encoder_output(2)
            attention_input(2)
            heads_norm(3)
            attended(0)
            encoder_output(3)
            experts_input(0)
            attention_input(3)
            attended(1)
            experts_input(1)
            route(0)
            attended(2)
            experts_input(2)
            choose(0)
            route(1)
            attended(3)
            choose(1)
            experts_input(3)
            for j in range(NT):
                grouped_low(j)
                if j == 2: route(2)
                if j == 4: choose(2)
                if j == 6: route(3)
                if j == 8: choose(3)
                if j: add_experts(j - 1)
            add_experts(NT - 1)

        @block.gpsimd
        def _(pool):
            def fold_matrix(gw):
                pool.tensor_copy(lncol[:, 0:1], cols[:, bass.ds(ROW_LNS + gw, 1)])
                pool.tensor_copy(lncol[:, 1:2], cols[:, bass.ds(ROW_LNB + gw, 1)]).then_inc(lncol_ready, 1)
                apart(pool, w1_ready, gw)
                apart(pool, lncol_ready, gw + 1)
                pool.tensor_scalar(fold_t[:, 1:P], K[:, C_FOLD + 1:C_FOLD + P], lncol[:, 0:1], None, ALU.mult)
                pool.tensor_copy(fold_t[:, 0:1], lncol[:, 1:2]).then_inc(fold_ready, 1)

            def normaliser(n, i, eps):
                at_least(pool, mv_ready, n + 1)
                pool.tensor_tensor(veps[i][:, :], mv[i][:, :, 1], eps[:, :], ALU.add).then_inc(veps_ready, 1)
                at_least(pool, veps_ready, n + 1)
                at_least(pool, z_ready, n - 1)
                pool.tensor_tensor(rstd[i][:, :], veps[i][:, :], half[:, :], ALU.pow).then_inc(rstd_ready, 1)

            def head_sums(b):
                pool.wait_ge(x_updated, (NG - 2) * B + b + 1)
                for h in range(1, H):
                    pool.tensor_tensor(h0[:, b, :], X[:, 0, b, :] if h == 1 else h0[:, b, :], X[:, h, b, :],
                                       ALU.add).then_inc(summed, 1)
                    if h < H - 1:
                        pool.wait_ge(summed, (H - 1) * b + h)

            def step(g, j):
                now, nxt2, nxt3 = (unit(g, j, a) for a in (0, 2, 3))
                gw = next_pair(g)
                if j == 0 and gw is not None:
                    fold_matrix(gw)
                if j == 1 and gw is not None:
                    pool.tensor_copy(bias3[:, :], cols[:, 0:3 * NG].rearrange("p (k g) -> p g k", k=3)[:, bass.ds(gw, 1), :]
                                     .rearrange("p o k -> p (o k)")).then_inc(bias3_ready, 1)
                    at_least(pool, bias3_ready, gw + 1)
                    at_least(pool, w1_copied, gw + 1)
                    pool.tensor_tensor(w_til[:, :, 0], w_til[:, :, 0], bias3[:, :], ALU.add).then_inc(w_til_ready, 1)
                if last_pair(g):
                    head_sums(j)
                if nxt3:
                    normaliser(nxt3[2], nxt3[1] % 2, eps_in)
                if isinstance(g, int) and nxt3 and nxt3[0] == 0:
                    b = nxt3[1]
                    pool.wait_ge(x_ready, b + 1)
                    for h in range(1, H):
                        ins = pool.tensor_copy(X[:, h, b, :], X[:, 0, b, :])
                    ins.then_inc(x_copied, 1)
                if isinstance(g, int) and g == 0:
                    q = slice(4 * j, 4 * j + 4)
                    if j == 0:
                        pool.wait_ge(ld_tail, 64)
                        pool.wait_ge(eb_ready, 1)
                    pool.tensor_tensor(ew[:, q, 1:P], ew[:, q, 1:P], ew[:, q, 0:1].to_broadcast([P, 4, P - 1]),
                                       ALU.subtract).then_inc(ew_sub, 1)
                    pool.wait_ge(ew_sub, j + 1)
                    pool.tensor_copy(ew[:, q, 0], eb_cols[:, q]).then_inc(ew_folded, 1)

            pool.wait_ge(setup, 1)
            pool.wait_ge(cols_ready, 1)
            run_steps(step)(pool)
            for n, (b, what) in enumerate(NORMS, NU):
                pool.wait_ge(mv_ready, n + 1)
                pool.tensor_tensor(veps[n % 2][:, :], mv[n % 2][:, :, 1], (eps_sum if what == "heads" else eps_in)[:, :],
                                   ALU.add).then_inc(veps_ready, 1)
                pool.wait_ge(veps_ready, n + 1)
                pool.tensor_tensor(rstd[n % 2][:, :], veps[n % 2][:, :], half[:, :], ALU.pow).then_inc(rstd_ready, 1)


_INS = ["x", "fside_BS_event_times", "mask_BS_i1_0", "L0_tok_type_emb", "L0_tok_Wq", "L0_tok_bq", "L0_tok_Wk",
        "L0_tok_bk", "L0_tok_Wv", "L0_tok_bv", "L0_tok_Wo", "L0_tok_bo", "L0_tok_ln_scale", "L0_tok_ln_bias",
        "L0_tok_final_scale", "L0_tok_final_bias", "L0_ffn_switch_w", "L0_ffn_switch_b", "L0_ffn_expert_w",
        "L0_ffn_expert_b"]


def kernel(**inputs):
    import concourse.bacc as bacc
    from concourse.bass_utils import run_bass_kernel_spmd

    nc = bacc.Bacc("TRN2", target_bir_lowering=False, num_devices=1)
    arrays, args = {}, []
    for name in _INS:
        a = np.ascontiguousarray(inputs[name])
        arrays[f"in_{name}"] = a
        args.append(nc.dram_tensor(f"in_{name}", a.shape, mybir.dt.from_np(a.dtype), kind="ExternalInput").ap())
    const = shape_constants()
    arrays["in_const"] = const
    args.append(nc.dram_tensor("in_const", const.shape, F32, kind="ExternalInput").ap())
    args.append(nc.dram_tensor("out_h", (B, S, P), F32, kind="ExternalOutput").ap())
    tower(nc, *args)
    r = run_bass_kernel_spmd(nc, [arrays], core_ids=[0])
    return r.results[0]["out_h"]
```

```python
from contextlib import ExitStack

import numpy as np

import concourse.bass as bass
from concourse import mybir

F32 = mybir.dt.float32
F32R = mybir.dt.float32r
BF16 = mybir.dt.bfloat16
I32 = mybir.dt.int32
U32 = mybir.dt.uint32
ALU = mybir.AluOpType
ACT = mybir.ActivationFunctionType
AX = mybir.AxisListType

P = 128
B, S = 4, 512
NC = S // P
NT = B * NC
H, L, V, E = 4, 4, 32, 16
NG = H * L
NU = NG * B
CAP = int(1.2 * B * S / E)
EPS = 1e-5
NEG = -1e9
SCALE = 1.0 / np.sqrt(P)
BIG = 1.5 * 2.0 ** 23
TWO_PI = 2.0 * np.pi
PI1 = 6.28125
PI2 = float(np.float32(np.round((TWO_PI - PI1) * 2 ** 20) / 2 ** 20))
PI3 = float(TWO_PI - PI1 - PI2)
PI_MAX = 3.1415925

NORMS = [(0, "heads"), (0, "y"), (1, "heads"), (1, "y"), (2, "heads"), (2, "y"), (3, "heads"), (0, "x3"),
         (3, "y"), (1, "x3"), (2, "x3"), (3, "x3")]

ROWS = [(0, "y"), (1, "y"), (2, "y"), (0, "x3"), (3, "y"), (1, "x3"), (2, "x3"), (3, "x3")]

TURNS = [(0, "y"), (1, "y"), (2, "y"), (0, "x3"), (3, "y"), (1, "x3"), (2, "x3"), (3, "x3")]

ROW_BQ, ROW_BK, ROW_BV, ROW_LNB, ROW_LNS, ROW_EB, ROW_SW, ROW_END = 0, 16, 32, 48, 64, 80, 96, 112
C_ID, C_IOTA, C_DIV, C_FOLD, C_TRI, C_END = 0, 128, 145, 209, 337, 465


def shape_constants():
    c = np.zeros((P, C_END), np.float32)
    c[:, C_ID:C_ID + P] = np.eye(P)
    fold = np.eye(P)
    fold[0, 1:] = -1.0
    fold[:, 0] = 0.0
    c[:, C_FOLD:C_FOLD + P] = fold
    c[:, C_TRI:C_TRI + P] = np.triu(np.ones((P, P)))
    rate = (2.0 * np.arange(P // 2)).astype(np.float32) * np.float32(-np.log(10000.0) / P)
    c[:, C_DIV:C_DIV + P // 2] = np.exp(rate)
    c[:, C_IOTA:C_IOTA + E] = np.arange(E)
    c[:, C_IOTA + E] = np.arange(P)
    return c


def tower(nc, ids, times, mask, type_emb, Wq, bq, Wk, bk, Wv, bv, Wo, bo, ln_scale, ln_bias,
          final_scale, final_bias, switch_w, switch_b, expert_w, expert_b, const, out):
    with ExitStack() as ctx:
        def sb(name, shape, dt=F32):
            return ctx.enter_context(nc.sbuf_tensor(name, shape, dt))

        def sem(name):
            return ctx.enter_context(nc.semaphore(name))

        bank = [ctx.enter_context(nc.psum_tensor(f"bank{i}", [P, 512], F32)) for i in range(8)]
        SC = bank[0:2]
        SA = bank[2:4]
        TB = bank[4]
        XB = bank[5]
        OB = [t[:, 0:258].rearrange("p (c d) -> p c d", c=2) for t in bank[6:8]]
        EW = [XB, XB, bank[2], bank[3]]
        EMB = [bank[i] for i in (1, 2, 6, 7)]
        LOGIT = TB[:, 0:NC * E].rearrange("p (c e) -> p c e", e=E)
        CUM = TB[:, 0:NC * E].rearrange("p (c e) -> p c e", e=E)

        K = sb("K", [P, C_END])
        ident = K[:, C_ID:C_ID + P]
        negident = sb("negident", [P, P], BF16)
        tri = sb("tri", [P, P], BF16)
        ones = sb("ones", [P, P], BF16)
        rows = sb("rows", [ROW_END, P])
        time_rows = sb("time_rows", [NT, P])
        mask_rows = sb("mask_rows", [NT, P])
        time_cols = sb("time_cols", [P, NT])
        mask_cols = sb("mask_cols", [P, NT])
        cols = sb("cols", [P, ROW_END])
        mask_i = sb("mask_i", [NT, P], I32)
        mask_b = sb("mask_b", [P, B * S], I32)
        key_mask = sb("key_mask", [P, B, S])
        masked_all = sb("masked_all", [P, B])
        some_key = sb("some_key", [P, B])
        key_bias = sb("key_bias", [P, NT])
        fin_s = sb("fin_s", [P, P])
        fin_b = sb("fin_b", [P, P])
        sw_b = sb("sw_b", [P, 1])
        half = sb("half", [P, NC])
        eps_in = sb("eps_in", [P, NC])
        eps_sum = sb("eps_sum", [P, NC])
        ids_b = sb("ids_b", [V, B * S], I32)
        onehot = sb("onehot", [V, B * S])
        emb = sb("emb", [V, P])
        half_pi = sb("half_pi", [P, 1])
        wave = sb("wave", [P, B, S])
        X = sb("X", [P, H, B, S])
        w_raw = sb("w_raw", [P, 4, P])
        bo_row = sb("bo_row", [1, P])
        fold_t = sb("fold_t", [P, P])
        lncol = sb("lncol", [P, 2])
        bias3 = sb("bias3", [P, 3])
        w_til = sb("w_til", [P, 3, P])
        g_hi = sb("g_hi", [P, P], F32R)
        g_lo = sb("g_lo", [P, P], F32R)
        wvo = sb("wvo", [P, P])
        stats = [sb(f"stats{i}", [P, NC, 6]) for i in range(2)]
        mv = [sb(f"mv{i}", [P, NC, 2]) for i in range(2)]
        veps = [sb(f"veps{i}", [P, NC]) for i in range(2)]
        rstd = [sb(f"rstd{i}", [P, NC]) for i in range(2)]
        z = [sb(f"z{i}", [P, NC, P]) for i in range(2)]
        zT = [sb(f"zT{i}", [P, S]) for i in range(4)]
        zh = [sb(f"zh{i}", [P, S], F32R) for i in range(4)]
        zl = [sb(f"zl{i}", [P, S], F32R) for i in range(4)]
        th = [sb(f"th{i}", [P, S], F32R) for i in range(2)]
        tl = [sb(f"tl{i}", [P, S], F32R) for i in range(2)]
        val = [sb(f"val{i}", [P, NC, P + 1]) for i in range(4)]
        mcol = sb("mcol", [P, NC], BF16)
        prob = [sb(f"prob{i}", [P, S]) for i in range(NC)]
        rsum = sb("rsum", [P, NC])
        h0 = sb("h0", [P, B, S])
        h1 = sb("h1", [P, NT, P])
        angle = h1[:, 0:NT // 2, :].rearrange("p j (a i) -> p (j a) i", a=2)
        turns = h1[:, NT // 2:NT, :].rearrange("p j (a i) -> p (j a) i", a=2)
        x3 = sb("x3", [P, NT, P])
        x3_0 = sb("x3_0", [P, NT])
        factor_of = sb("factor_of", [P, len(NORMS), NC])
        shift_of = sb("shift_of", [P, len(NORMS), NC])
        square = sb("square", [P, B, NC, P], BF16)
        negsq = sb("negsq", [P, NC])
        logit = sb("logit", [P, NT, E])
        lexp = sb("lexp", [P, NT, E])
        top8 = sb("top8", [P, NT, 8])
        idx8 = sb("idx8", [P, NT, 8], U32)
        route1 = sb("route1", [P, NT, E], BF16)
        lsum = sb("lsum", [P, NT])
        rprob = sb("rprob", [P, NT])
        gate = sb("gate", [P, NT, E])
        group = sb("group", [P, NT, 4])
        member = sb("member", [P, NT, 4])
        drop = sb("drop", [P, NT])
        ew = sb("ew", [P, E, P])
        eh = sb("eh", [P, E, P], F32R)
        el = sb("el", [P, E, P], F32R)
        xg = [sb(f"xg{i}", [P, 4, P]) for i in range(2)]
        acc = [sb(f"acc{i}", [P, P]) for i in range(2)]
        acc_out = [sb(f"acc_out{i}", [P, P]) for i in range(2)]

        ld_times, ld_const, ld_ids, ld_rows, ld_mask, ld_tail, ld_w = map(
            sem, "ld_times ld_const ld_ids ld_rows ld_mask ld_tail ld_w".split())
        stored = [sem("stored_even"), sem("stored_odd")]
        mask_rows_ready, times_turned, times_ready = map(sem, "mask_rows_ready times_turned times_ready".split())
        rows_ready, cols_turned, cols_ready = map(sem, "rows_ready cols_turned cols_ready".split())
        onehot_ready, emb_ready, angle_ready, turns_ready, wave_ready = map(
            sem, "onehot_ready emb_ready angle_ready turns_ready wave_ready".split())
        x_ready, some_ready, mask_ready, setup = map(
            sem, "x_ready some_ready mask_ready setup".split())
        x_copied = [sem(f"x_copied{b}") for b in range(B)]
        lncol_ready, fold_ready, w1_ready, w1_copied = map(sem, "lncol_ready fold_ready w1_ready w1_copied".split())
        bias3_ready, w_til_ready, w2_ready, w2_copied, w_ready = map(
            sem, "bias3_ready w_til_ready w2_ready w2_copied w_ready".split())
        stats_ready, mv_ready, veps_ready, rstd_ready, z_ready = map(
            sem, "stats_ready mv_ready veps_ready rstd_ready z_ready".split())
        zt_ready, zt_copied, zhi_ready, zlo_ready = map(sem, "zt_ready zt_copied zhi_ready zlo_ready".split())
        v_ready, v_copied, t_ready, th_ready = map(sem, "v_ready v_copied t_ready th_ready".split())
        sa_ready, max_ready, inj_ready, row_ready, tl_ready = map(
            sem, "sa_ready max_ready inj_ready row_ready tl_ready".split())
        sc_ready, exp_done, av_done, rsum_ready, x_updated = map(
            sem, "sc_ready exp_done av_done rsum_ready x_updated".split())
        ew_sub, ew_folded, ew_turned, ew_high, ew_ready = map(sem, "ew_sub ew_folded ew_turned ew_high ew_ready".split())
        shift_ready, rows_normal = sem("shift_ready"), sem("rows_normal")
        summed, square_ready, turned, turned_copied = map(sem, "summed square_ready turned turned_copied".split())
        tail_sc, tail_exp, tail_av, h1_ready, x3_0_ready = map(sem, "tail_sc tail_exp tail_av h1_ready x3_0_ready".split())
        logit_ready, lshift_ready, lexp_ready, routed, cum_ready, group_ready = map(
            sem, "logit_ready lshift_ready lexp_ready routed cum_ready group_ready".split())
        xg_ready, grouped, grouped_high, grouped_ready, expert_out, acc_ready = map(
            sem, "xg_ready grouped grouped_high grouped_ready expert_out acc_ready".split())
        chain = sem("chain")
        pool_chain = sem("pool_chain")
        passed = sem("passed")

        def unit(g, j, ahead):
            gg, b = g + (j + ahead) // B, (j + ahead) % B
            if isinstance(gg, int) and not 0 <= gg < NG:
                return None
            return gg, b, gg * B + b

        def next_pair(g):
            return None if isinstance(g, int) and not 0 <= g < NG - 1 else g + 1

        def last_pair(g):
            return isinstance(g, int) and g == NG - 1

        def at_least(eng, s, n):
            if not isinstance(n, int) or n > 0:
                eng.wait_ge(s, n)

        def apart(eng, s, n):
            at_least(eng, s, n)
            if not isinstance(n, int):
                eng.sem_inc(passed, 1)

        def run_steps(step):
            def run(eng):
                for g in (-1, 0):
                    for j in range(B):
                        step(g, j)
                with eng.Fori(1, NG - 1) as g:
                    for j in range(B):
                        step(g, j)
                for j in range(B):
                    step(NG - 1, j)
                step(NG, 0)
            return run

        def encode_turns(eng, after, b):
            js = slice(b * NC, (b + 2) * NC)
            n = 2 * NC
            a, k = angle[:, js, :], turns[:, js, :]
            after(eng.tensor_tensor(a, time_cols[:, js].unsqueeze(2).to_broadcast([P, n, P // 2]),
                                    K[:, C_DIV:C_DIV + P // 2].unsqueeze(1).to_broadcast([P, n, P // 2]), ALU.mult))
            after(eng.tensor_scalar(k, a, float(1.0 / TWO_PI), BIG, ALU.mult, ALU.add))
            after(eng.tensor_scalar(k, k, BIG, None, ALU.subtract))

        block = ctx.enter_context(nc.Block())

        @block.sync
        def _(sp):
            sp.dma_start(time_rows[:, :], times.rearrange("b (c p) -> (b c) p", p=P)).then_inc(ld_times, 16)
            sp.dma_start(mask_i[:, :], mask.rearrange("b (c p) -> (b c) p", p=P)).then_inc(ld_times, 16)
            for a, at in ((bq, ROW_BQ), (bk, ROW_BK), (bv, ROW_BV), (ln_bias, ROW_LNB), (ln_scale, ROW_LNS)):
                sp.dma_start(rows[at:at + NG, :], a.rearrange("h l d -> (h l) d")).then_inc(ld_rows, 16)
            sp.dma_start(rows[ROW_EB:ROW_EB + E, :], expert_b).then_inc(ld_rows, 16)
            sp.dma_start(rows[ROW_SW:ROW_SW + E, :], switch_w).then_inc(ld_rows, 16)
            sp.dma_start(sw_b[ROW_SW:ROW_SW + E, :], switch_b.rearrange("(e a) -> e a", a=1)).then_inc(ld_rows, 16)

            def load_pair(gw):
                at_least(sp, w_ready, gw)
                i = (gw % H) * L + gw // H
                for k, w in enumerate((Wq, Wk, Wv, Wo)):
                    v = w.rearrange("h l a b -> (h l) a b")
                    sp.dma_start(w_raw[:, k, :], v[bass.ds(i, 1), :, :].rearrange("o a b -> a (o b)")).then_inc(ld_w, 16)
                sp.dma_start(bo_row[:, :], bo.rearrange("h l d -> (h l) d")[bass.ds(i, 1), :]).then_inc(ld_w, 16)

            def step(g, j):
                gw = next_pair(g)
                if j == 0 and gw is not None:
                    load_pair(gw)
                if isinstance(g, int) and g == -1 and j == 0:
                    sp.dma_start(ew[:, :, :], expert_w.rearrange("e f d -> f e d")).then_inc(ld_tail, 16)
                    sp.dma_start(fin_s[:, :], final_scale.unsqueeze(0).to_broadcast([P, P])).then_inc(ld_tail, 16)
                    sp.dma_start(fin_b[:, :], final_bias.unsqueeze(0).to_broadcast([P, P])).then_inc(ld_tail, 16)

                if isinstance(g, int) and g == -1:
                    sp.wait_ge(x_ready, j + 1)
                    sp.dma_start(X[:, 1:H, j, :], X[:, 0:1, j, :].to_broadcast([P, H - 1, S])).then_inc(x_copied[j], 16)

            sp.dma_start(mask_b[:, :], mask.rearrange("b s -> (b s)").unsqueeze(0).to_broadcast([P, B * S])).then_inc(ld_mask, 16)
            load_pair(0)
            run_steps(step)(sp)
            for j in range(NT):
                sp.wait_ge(acc_ready, j + 1)
                sp.dma_start(out.rearrange("b (c p) d -> (b c) p d", p=P)[j], acc_out[j % 2][:, :]).then_inc(stored[j % 2], 16)
            for s in stored:
                sp.wait_ge(s, 16 * NT // 2)

        @block.tensor
        def _(pe):
            pe.wait_ge(ld_times, 32)
            pe.wait_ge(ld_const, 16)
            pe.transpose(bank[0][:, 0:NT], time_rows[:, :], K[0:NT, C_ID:C_ID + NT])
            pe.wait_ge(mask_rows_ready, 1)
            pe.transpose(bank[0][:, NT:2 * NT], mask_rows[:, :], K[0:NT, C_ID:C_ID + NT]).then_inc(times_turned, 1)
            pe.wait_ge(rows_ready, 1)
            pe.transpose(TB[:, 0:ROW_END], rows[:, :], K[0:ROW_END, C_ID:C_ID + ROW_END]).then_inc(cols_turned, 1)
            def embeddings(b):
                for c in range(NC):
                    mm = pe.matmul(EMB[b][:, c * P:(c + 1) * P],
                                   onehot[:, (b * NC + c) * P:(b * NC + c + 1) * P], emb[:, :],
                                   start=True, stop=True)
                mm.then_inc(emb_ready, 1)

            def scores(u, kc):
                g, b, n = u
                at_least(pe, exp_done, NC * n + kc - 1)
                if kc == 0:
                    at_least(pe, tl_ready, n + 1)
                ks = slice(kc * P, (kc + 1) * P)
                o = SC[kc % 2][:, :]
                pe.matmul(o, zh[b][:, ks], th[b % 2][:, :], start=True, stop=False)
                pe.matmul(o, zh[b][:, ks], tl[b % 2][:, :], start=False, stop=False)
                pe.matmul(o, zl[b][:, ks], th[b % 2][:, :], start=False, stop=True).then_inc(sc_ready, 1)

            def times_values(u, kc):
                g, b, n = u
                at_least(pe, exp_done, NC * n + kc + 1)
                if kc == 0:
                    at_least(pe, x_updated, n)
                    if isinstance(g, int) and n == 0:
                        pe.wait_ge(x_ready, B)
                for c in range(NC):
                    mm = pe.matmul(OB[c // 2][:, c % 2, :], prob[kc][:, c * P:(c + 1) * P],
                                   val[b][:, kc, :], start=(kc == 0 and c % 2 == 0), stop=(kc == NC - 1),
                                   skip_group_check=True)
                mm.then_inc(av_done, 1)

            def rough_scores(u, c):
                g, b, n = u
                if c == 0:
                    at_least(pe, th_ready, n + 1)
                    if isinstance(g, int) and n == 0:
                        pe.wait_ge(x_ready, 2)
                at_least(pe, max_ready, NC * n + c - 1)
                pe.matmul(SA[c % 2][:, :], th[b % 2][:, c * P:(c + 1) * P], zh[b][:, :],
                          start=True, stop=True).then_inc(sa_ready, 1)

            def turn_z(u):
                g, b, n = u
                at_least(pe, z_ready, n + 1)
                at_least(pe, v_copied, n)
                for c in range(NC):
                    mm = pe.transpose(XB[:, c * P:(c + 1) * P], z[b % 2][:, c, :], ident)
                mm.then_inc(zt_ready, 1)

            def values(u):
                g, b, n = u
                at_least(pe, zt_copied, n + 1)
                at_least(pe, w_ready, g + 1)
                for c in range(NC):
                    mm = pe.matmul(XB[:, c * P:(c + 1) * P], zT[b][:, c * P:(c + 1) * P], wvo[:, :],
                                   start=True, stop=True)
                mm.then_inc(v_ready, 1)

            def project(u):
                g, b, n = u
                at_least(pe, zlo_ready, n + 1)
                at_least(pe, tl_ready, n)
                pe.matmul(TB[:, :], g_hi[:, :], zh[b][:, :], start=True, stop=False)
                pe.matmul(TB[:, :], g_hi[:, :], zl[b][:, :], start=False, stop=False)
                pe.matmul(TB[:, :], g_lo[:, :], zh[b][:, :], start=False, stop=True).then_inc(t_ready, 1)

            def inject(u):
                g, b, n = u
                at_least(pe, max_ready, NC * (n + 1))
                for c in range(NC):
                    mm = pe.matmul(TB[0:1, c * P:(c + 1) * P], mcol[:, c:c + 1], negident[:, :],
                                   start=False, stop=True, skip_group_check=True)
                mm.then_inc(inj_ready, 1)

            def fold_1(gw, n2):
                at_least(pe, fold_ready, gw + 1)
                at_least(pe, ld_w, 80 * (gw + 1))
                if n2:
                    at_least(pe, zt_copied, n2[2] + 1)
                for k in range(3):
                    mm = pe.matmul(XB[:, k * P:(k + 1) * P], w_raw[:, k, :], fold_t[:, :], start=True, stop=True)
                mm.then_inc(w1_ready, 1)

            def fold_2(gw):
                at_least(pe, w_til_ready, gw + 1)
                at_least(pe, v_copied, gw * B)
                pe.matmul(XB[:, 0:P], w_til[:, 0, :], w_til[:, 1, :], start=True, stop=True)
                pe.matmul(XB[:, P:2 * P], w_til[:, 2, :], w_raw[:, 3, :], start=True, stop=True).then_inc(w2_ready, 1)

            def turn_rows(b, what):
                i = TURNS.index((b, what))
                if i == 0:
                    pe.wait_ge(ew_ready, 2)
                pe.wait_ge(rows_normal, ROWS.index((b, what)) + 1)
                if i:
                    pe.wait_ge(turned_copied, i)
                for c in range(NC):
                    mm = pe.transpose(XB[:, c * P:(c + 1) * P], val[b][:, c, 0:P] if what == "y" else x3[:, b * NC + c, :], ident)
                mm.then_inc(turned, 1)

            def turn_experts(q):
                pe.wait_ge(ew_folded, 4)
                if q == 1:
                    pe.wait_ge(ew_ready, 1)
                if q == 2:
                    pe.wait_ge(max_ready, NC * NU)
                for k in range(4):
                    mm = pe.transpose(EW[q][:, k * P:(k + 1) * P], ew[:, 4 * q + k, :], ident)
                mm.then_inc(ew_turned, 1)

            def step(g, j):
                last, now, nxt, nxt2 = (unit(g, j, a) for a in (-1, 0, 1, 2))
                gw = next_pair(g)
                if j == 2 and gw is not None: fold_2(gw)
                if isinstance(g, int) and g == NG:
                    turn_rows(0, "y")
                if now: scores(now, 0)
                if last: times_values(last, 2)
                if nxt: rough_scores(nxt, 0)
                if j == 2 and gw is not None or isinstance(g, int) and (g, j) == (-1, 2):
                    at_least(pe, w_ready, g + 2)
                if last_pair(g) and j >= 2: turn_experts(j - 2)
                if nxt2: turn_z(nxt2)
                if nxt: rough_scores(nxt, 1)
                if last: times_values(last, 3)
                if nxt: rough_scores(nxt, 2)
                if nxt: rough_scores(nxt, 3)
                if now: scores(now, 1)
                if j == 1 and gw is not None:
                    at_least(pe, v_copied, gw * B - 1)
                    fold_1(gw, nxt2)
                if now: scores(now, 2)
                if nxt: inject(nxt)
                if nxt2:
                    if j == 1 and gw is not None:
                        at_least(pe, w1_copied, g + 2)
                    values(nxt2)
                if last_pair(g) and j == 3:
                    turn_experts(2)
                    turn_experts(3)
                if now: scores(now, 3)
                if now: times_values(now, 0)
                if now: times_values(now, 1)
                if nxt2: project(nxt2)

            pe.wait_ge(onehot_ready, 1)
            embeddings(0)
            fold_1(0, None)
            embeddings(1)
            fold_2(0)
            embeddings(2)
            embeddings(3)
            run_steps(step)(pe)

            def tail_values(b, kc):
                pe.wait_ge(tail_exp, NC * b + kc + 1)
                if kc == 0:
                    pe.wait_ge(*((h1_ready, b) if b else (x_updated, NU)))
                for c in range(NC):
                    mm = pe.matmul(OB[c // 2][:, c % 2, :], prob[kc][:, c * P:(c + 1) * P], val[b][:, kc, :],
                                   start=(kc == 0 and c % 2 == 0), stop=(kc == NC - 1), skip_group_check=True)
                mm.then_inc(tail_av, 1)

            def tail_scores(b, kc):
                if kc == 0:
                    pe.wait_ge(square_ready, b + 1)
                    pe.wait_ge(turned_copied, TURNS.index((b, "y")) + 1)
                if NC * b + kc >= 2:
                    pe.wait_ge(tail_exp, NC * b + kc - 1)
                pe.matmul(SC[kc % 2][:, :], ones[:, :], square[:, b, :, :], start=True, stop=False)
                pe.matmul(SC[kc % 2][:, :], zT[b][:, kc * P:(kc + 1) * P], zT[b][:, :],
                          start=False, stop=True).then_inc(tail_sc, 1)

            def attend(b):
                tail_scores(b, 1)
                if b == 2: logits(0)
                tail_values(b, 0)
                tail_scores(b, 2)
                if b < B - 1: turn_rows(b + 1, "y")
                tail_values(b, 1)
                tail_scores(b, 3)
                if b == 3: logits(1)
                tail_values(b, 2)
                if b < B - 1: tail_scores(b + 1, 0)
                if b == B - 1: turn_groups(0)
                tail_values(b, 3)

            def logits(b):
                pe.wait_ge(turned_copied, TURNS.index((b, "x3")) + 1)
                if b:
                    pe.wait_ge(group_ready, b)
                for c in range(NC):
                    mm = pe.matmul(LOGIT[:, c, :], zT[b][:, c * P:(c + 1) * P], cols[:, ROW_SW:ROW_SW + E],
                                   start=True, stop=True)
                mm.then_inc(logit_ready, 1)

            def count_routes(b):
                pe.wait_ge(routed, b + 1)
                pe.matmul(CUM, tri[:, :], route1[:, b * NC:(b + 1) * NC, :], start=True, stop=True)
                for i in range((b + 1) * NC - 1):
                    c = max(i + 1 - b * NC, 0)
                    mm = pe.matmul(CUM[:, c:NC, :], ones[:, :], route1[:, i:i + 1, :].to_broadcast([P, NC - c, E]),
                                   start=False, stop=True, skip_group_check=True)
                mm.then_inc(cum_ready, 1)

            def turn_groups(j):
                if j < NT:
                    pe.wait_ge(xg_ready, j + 1)
                    if j == 0:
                        pe.wait_ge(ew_ready, 4)
                    if j >= 2:
                        pe.wait_ge(grouped_ready, j - 1)
                    for a in range(4):
                        mm = pe.transpose(SA[j % 2][:, a * P:(a + 1) * P], xg[j % 2][:, a, :], ident)
                    mm.then_inc(grouped, 1)

            def experts(j):
                pe.wait_ge(grouped_ready, j + 1)
                if j < 2:
                    pe.wait_ge(tail_exp, NC * B)
                else:
                    pe.wait_ge(acc_ready, j - 1)
                o = SC[j % 2][:, :]
                for a in range(4):
                    js, es = slice(a * P, (a + 1) * P), slice(4 * a, 4 * a + 4)
                    pe.matmul(o, th[j % 2][:, js], eh[:, es, :], start=(a == 0), stop=False)
                    pe.matmul(o, th[j % 2][:, js], el[:, es, :], start=False, stop=False)
                    mm = pe.matmul(o, tl[j % 2][:, js], eh[:, es, :], start=False, stop=(a == 3))
                mm.then_inc(expert_out, 1)

            tail_scores(0, 0)
            attend(0)
            attend(1)
            turn_rows(0, "x3")
            attend(2)
            turn_rows(1, "x3")
            count_routes(0)
            attend(3)
            turn_rows(2, "x3")
            count_routes(1)
            for j in range(NT):
                turn_groups(j + 1)
                experts(j)
                if j == 1: logits(2)
                if j == 3: turn_rows(3, "x3")
                if j == 4: count_routes(2)
                if j == 5: logits(3)
                if j == 7: count_routes(3)

        @block.scalar
        def _(act):
            act.dma_start(K[:, :], const).then_inc(ld_const, 16)
            act.dma_start(ids_b[:, :], ids.rearrange("b s -> (b s)").unsqueeze(0).to_broadcast([V, B * S])).then_inc(ld_ids, 16)
            act.dma_start(emb[:, :], type_emb).then_inc(ld_ids, 16)
            act.wait_ge(times_turned, 1)
            act.copy(time_cols[:, :], bank[0][:, 0:NT])
            act.copy(mask_cols[:, :], bank[0][:, NT:2 * NT]).then_inc(times_ready, 1)
            act.wait_ge(cols_turned, 1)
            act.copy(cols[:, 0:ROW_EB].rearrange("p (k l h) -> p k h l", l=L, h=H),
                     TB[:, 0:ROW_EB].rearrange("p (k h l) -> p k h l", l=L, h=H))
            act.copy(cols[:, ROW_EB:ROW_END], TB[:, ROW_EB:ROW_END]).then_inc(cols_ready, 1)

            def waves(b):
                act.wait_ge(angle_ready, b // 2 + 1)
                w = wave[:, b, :].rearrange("p (c i a) -> p c i a", c=NC, a=2)
                act.activation(w[:, :, :, 0], angle[:, b * NC:(b + 1) * NC, :], ACT.Sin)
                act.activation(w[:, :, :, 1], turns[:, b * NC:(b + 1) * NC, :], ACT.Sin, scale=-1.0, bias=half_pi[:, 0:1]).then_inc(wave_ready, 1)

            def copy_fold_1(gw):
                at_least(act, w1_ready, gw + 1)
                act.copy(w_til[:, :, :], XB[:, 0:3 * P].rearrange("p (k d) -> p k d", k=3)).then_inc(w1_copied, 1)

            def copy_fold_2(gw):
                at_least(act, w2_ready, gw + 1)
                act.activation(g_hi[:, :], XB[:, 0:P], ACT.Identity, scale=float(SCALE)).then_inc(w2_copied, 1)
                act.copy(wvo[:, :], XB[:, P:2 * P]).then_inc(w2_copied, 1)

            def exps(u, kc):
                g, b, n = u
                at_least(act, sc_ready, NC * n + kc + 1)
                at_least(act, av_done, NC * (n - 1) + kc + 1)
                act.activation(prob[kc][:, :], SC[kc % 2][:, :], ACT.Exp,
                               bias=key_bias[:, b * NC + kc:b * NC + kc + 1]).then_inc(exp_done, 1)

            def step(g, j):
                now, nxt, nxt2 = (unit(g, j, a) for a in (0, 1, 2))
                gw = next_pair(g)
                if j == 2 and gw is not None:
                    copy_fold_2(gw)
                if isinstance(g, int) and (g, j) == (0, 0):
                    act.wait_ge(mask_ready, 1)
                if isinstance(g, int) and g == NG:
                    normal_rows(0, "y")
                    turned_copy(0, 0)
                if now: exps(now, 0)
                if last_pair(g) and j >= 2: experts_high(j - 2)
                if nxt2:
                    at_least(act, zt_ready, nxt2[2] + 1)
                    act.copy(zh[nxt2[1]][:, :], XB[:, :]).then_inc(zhi_ready, 1)
                    act.copy(zT[nxt2[1]][:, :], XB[:, :]).then_inc(zt_copied, 1)
                if now: exps(now, 1)
                if j == 1 and gw is not None:
                    copy_fold_1(gw)
                if now: exps(now, 2)
                if nxt:
                    at_least(act, inj_ready, nxt[2] + 1)
                    act.activation(th[nxt[1] % 2][0:1, :], TB[0:1, :], ACT.Identity,
                                   scale=some_key[0:1, nxt[1]:nxt[1] + 1]).then_inc(row_ready, 1)
                if last_pair(g) and j == 3:
                    experts_high(2)
                    experts_high(3)
                if nxt2:
                    at_least(act, v_ready, nxt2[2] + 1)
                    act.copy(val[nxt2[1]][:, :, 0:P], XB[:, :].rearrange("p (c d) -> p c d", c=NC)).then_inc(v_copied, 1)
                if now: exps(now, 3)
                if nxt2:
                    if isinstance(g, int) and nxt2[2] == 0:
                        act.wait_ge(some_ready, 1)
                    at_least(act, t_ready, nxt2[2] + 1)
                    act.activation(th[nxt2[1] % 2][:, :], TB[:, :], ACT.Identity,
                                   scale=some_key[:, nxt2[1]:nxt2[1] + 1]).then_inc(th_ready, 1)

            def normal_rows(b, what):
                act.wait_ge(shift_ready, ROWS.index((b, what)) + 1)
                i = NORMS.index((b, what))
                for c in range(NC):
                    if what == "y":
                        out_, in_ = val[b][:, c, 0:P], h0[:, b, c * P:(c + 1) * P]
                    else:
                        out_, in_ = x3[:, b * NC + c, 1:P], h1[:, b * NC + c, 1:P]
                    ins = act.activation(out_, in_, ACT.Identity, scale=factor_of[:, i, c:c + 1], bias=shift_of[:, i, c:c + 1])
                ins.then_inc(rows_normal, 1)

            def turned_copy(b, i):
                act.wait_ge(turned, i + 1)
                act.copy(zT[b][:, :], XB[:, :]).then_inc(turned_copied, 1)

            def experts_high(q):
                act.wait_ge(ew_turned, q + 1)
                act.copy(eh[:, 4 * q:4 * q + 4, :], EW[q][:, :].rearrange("p (k d) -> p k d", k=4)).then_inc(ew_high, 1)

            waves(0)
            waves(1)
            copy_fold_1(0)
            copy_fold_2(0)
            waves(2)
            waves(3)
            run_steps(step)(act)

            def attention_exps(b):
                for kc in range(NC):
                    act.wait_ge(tail_sc, NC * b + kc + 1)
                    if b:
                        act.wait_ge(tail_av, NC * (b - 1) + kc + 1)
                    act.activation(prob[kc][:, :], SC[kc % 2][:, :], ACT.Exp).then_inc(tail_exp, 1)
                    if b == B - 1 and kc == 1:
                        group_rows(0)
                    if kc == 1 and b < B - 1:
                        normal_rows(b + 1, "y")
                    if kc == 3 and 0 < b < B - 1:
                        normal_rows(b - 1, "x3")
                    if kc == 2 and b < B - 1:
                        turned_copy(b + 1, TURNS.index((b + 1, "y")))

            def route_exps(b):
                js = slice(b * NC, (b + 1) * NC)
                act.wait_ge(lshift_ready, b + 1)
                act.activation(lexp[:, js, :], lexp[:, js, :], ACT.Exp).then_inc(lexp_ready, 1)

            def group_rows(j):
                if j < NT:
                    act.wait_ge(group_ready, j // NC + 1)
                    if j % NC == 0:
                        act.wait_ge(rows_normal, ROWS.index((j // NC, "x3")) + 1)
                    for a in range(4):
                        ins = act.activation(xg[j % 2][:, a, :], x3[:, j, :], ACT.Identity, scale=group[:, j, a:a + 1])
                    ins.then_inc(xg_ready, 1)

            def high_rows(j):
                act.wait_ge(grouped, j + 1)
                if j >= 2:
                    act.wait_ge(expert_out, j - 1)
                act.copy(th[j % 2][:, :], SA[j % 2][:, :]).then_inc(grouped_high, 1)

            attention_exps(0)
            attention_exps(1)
            turned_copy(0, TURNS.index((0, "x3")))
            attention_exps(2)
            route_exps(0)
            turned_copy(1, TURNS.index((1, "x3")))
            attention_exps(3)
            normal_rows(2, "x3")
            high_rows(0)
            group_rows(1)
            route_exps(1)
            turned_copy(2, TURNS.index((2, "x3")))
            for j in range(NT):
                if j:
                    high_rows(j)
                group_rows(j + 2)
                if j == 2: normal_rows(3, "x3")
                if j == 3: route_exps(2)
                if j == 4: turned_copy(3, TURNS.index((3, "x3")))
                if j == 7: route_exps(3)

        @block.vector
        def _(dve):
            count = [0]

            def then(ins):
                count[0] += 1
                ins.then_inc(chain, 1)
                dve.wait_ge(chain, count[0])

            for t in z + [x3]:
                dve.memset(t[:, :, 0:1], 1.0)
            for t in val:
                dve.memset(t[:, :, P:P + 1], 1.0)
            dve.memset(half_pi[:, :], float(np.pi / 2))
            dve.memset(half[:, :], -0.5)
            dve.memset(eps_in[:, :], EPS)
            dve.memset(eps_sum[:, :], H * H * EPS)
            dve.memset(ones[:, :], 1.0)
            dve.wait_ge(ld_times, 32)
            dve.tensor_scalar(mask_rows[:, :], mask_i[:, :], 0, NEG, ALU.is_equal, ALU.mult).then_inc(mask_rows_ready, 1)
            dve.wait_ge(ld_const, 16)
            dve.tensor_copy(tri[:, :], K[:, C_TRI:C_TRI + P])
            dve.tensor_scalar(negident[:, :], ident, -1.0, None, ALU.mult).then_inc(setup, 1)

            def some_keys():
                then(dve.tensor_reduce(masked_all[:, :], key_mask[:, :, :], AX.X, ALU.max))
                dve.tensor_scalar(some_key[:, :], masked_all[:, :], 0.0, None, ALU.is_equal).then_inc(some_ready, 1)

            def masks():
                dve.wait_ge(some_ready, 1)
                for b in range(B):
                    dve.tensor_scalar(key_mask[:, b, :], key_mask[:, b, :], some_key[:, b:b + 1], None, ALU.mult)
                dve.tensor_tensor(key_bias[:, :].rearrange("p (b c) -> p b c", b=B),
                                  mask_cols[:, :].rearrange("p (b c) -> p b c", b=B),
                                  some_key[:, :].unsqueeze(2).to_broadcast([P, B, NC]), ALU.mult).then_inc(mask_ready, 1)

            def encode_angles(b):
                a, k = angle[:, b * NC:(b + 2) * NC, :], turns[:, b * NC:(b + 2) * NC, :]
                for part in (PI1, PI2, PI3):
                    then(dve.scalar_tensor_tensor(out=a, in0=k, scalar=-part, in1=a, op0=ALU.mult, op1=ALU.add))
                then(dve.tensor_scalar(a, a, PI_MAX, -PI_MAX, ALU.min, ALU.max))
                dve.scalar_tensor_tensor(out=k, in0=a, scalar=-1.0, in1=a, op0=ALU.mult, op1=ALU.max).then_inc(angle_ready, 1)

            dve.wait_ge(times_ready, 1)
            encode_turns(dve, then, 0)
            encode_angles(0)
            dve.wait_ge(ld_rows, 16 * 8)
            sw_rows = rows[ROW_SW:ROW_SW + E, :]
            then(dve.tensor_scalar(sw_rows[:, 1:P], sw_rows[:, 1:P], sw_rows[:, 0:1], None, ALU.subtract))
            dve.tensor_copy(sw_rows[:, 0:1], sw_b[ROW_SW:ROW_SW + E, :]).then_inc(rows_ready, 1)
            dve.wait_ge(ld_ids, 32)
            dve.tensor_scalar(onehot[:, :], ids_b[:, :], K[0:V, C_IOTA + E:C_IOTA + E + 1], None,
                              ALU.is_equal).then_inc(onehot_ready, 1)
            dve.wait_ge(ld_mask, 16)
            then(dve.tensor_scalar(key_mask[:, :, :].rearrange("p b s -> p (b s)"), mask_b[:, :], 0, NEG,
                                   ALU.is_equal, ALU.mult))

            def low_weights(gw):
                at_least(dve, w2_copied, 2 * (gw + 1))
                dve.scalar_tensor_tensor(out=g_lo[:, :], in0=XB[:, 0:P], scalar=float(SCALE), in1=g_hi[:, :].bitcast(F32),
                                         op0=ALU.mult, op1=ALU.subtract)
                dve.tensor_tensor(wvo[0:1, :], wvo[0:1, :], bo_row[:, :], ALU.add).then_inc(w_ready, 1)

            def maxima(u, c):
                g, b, n = u
                if c == 0:
                    apart(dve, inj_ready, n)
                apart(dve, sa_ready, NC * n + c + 1)
                sa = SA[c % 2][:, :]
                dve.tensor_tensor_reduce(out=sa, in0=sa, in1=key_mask[:, b, :], scale=1.0, scalar=-3e38,
                                         op0=ALU.add, op1=ALU.max, accum_out=mcol[:, c:c + 1]).then_inc(max_ready, 1)

            def row_stats(x, n, i):
                for c in range(NC):
                    ins = dve.bn_stats(stats[i][:, c, :], x[:, c * P:(c + 1) * P])
                ins.then_inc(stats_ready, 1)
                apart(dve, rstd_ready, n - 1)
                apart(dve, stats_ready, n + 1)
                for c in range(NC):
                    ins = dve.bn_aggr(mv[i][:, c, :], stats[i][:, c, :])
                ins.then_inc(mv_ready, 1)

            def step(g, j):
                last, now, nxt, nxt2, nxt3, nxt4 = (unit(g, j, a) for a in (-1, 0, 1, 2, 3, 4))
                gw = next_pair(g)
                if j == 2 and gw is not None:
                    low_weights(gw)
                if isinstance(g, int) and (g, j) == (-1, 3):
                    dve.wait_ge(mask_ready, 1)
                if nxt: maxima(nxt, 0)
                if nxt: maxima(nxt, 1)
                if nxt: maxima(nxt, 2)
                if nxt: maxima(nxt, 3)
                if last:
                    g_, b_, n_ = last
                    at_least(dve, av_done, NC * (n_ + 1))
                    dve.reciprocal(rsum[:, 0:2], OB[0][:, :, P])
                    dve.reciprocal(rsum[:, 2:4], OB[1][:, :, P]).then_inc(rsum_ready, 1)
                    at_least(dve, rsum_ready, n_ + 1)
                    if last_pair(g_):
                        dve.wait_ge(summed, (H - 1) * (b_ + 1))
                    for c in range(NC):
                        xs = h0[:, b_, c * P:(c + 1) * P] if last_pair(g_) else X[:, g_ % H, b_, c * P:(c + 1) * P]
                        ins = dve.scalar_tensor_tensor(out=xs, in0=OB[c // 2][:, c % 2, 0:P], scalar=rsum[:, c:c + 1],
                                                       in1=xs, op0=ALU.mult, op1=ALU.add)
                    ins.then_inc(x_updated, 1)
                if last_pair(g) and j >= 2: experts_low(j - 2)
                if nxt2:
                    at_least(dve, zt_copied, nxt2[2] + 1)
                    dve.tensor_tensor(zl[nxt2[1]][:, :], zT[nxt2[1]][:, :], zh[nxt2[1]][:, :].bitcast(F32),
                                      ALU.subtract).then_inc(zlo_ready, 1)
                if nxt:
                    at_least(dve, row_ready, nxt[2] + 1)
                    t = nxt[1] % 2
                    dve.scalar_tensor_tensor(out=tl[t][:, :], in0=TB[:, :], scalar=some_key[:, nxt[1]:nxt[1] + 1],
                                             in1=th[t][:, :].bitcast(F32), op0=ALU.mult, op1=ALU.subtract).then_inc(tl_ready, 1)
                if nxt3:
                    at_least(dve, rstd_ready, nxt3[2] + 1)
                    at_least(dve, zt_ready, nxt3[2] - 1)
                    for c in range(NC):
                        ins = dve.tensor_scalar(z[nxt3[1] % 2][:, c, 1:P], X[:, nxt3[0] % H, nxt3[1], c * P + 1:(c + 1) * P],
                                                mv[nxt3[1] % 2][:, c, 0:1], rstd[nxt3[1] % 2][:, c:c + 1],
                                                ALU.subtract, ALU.mult)
                    ins.then_inc(z_ready, 1)
                if isinstance(g, int) and g == -1:
                    dve.wait_ge(wave_ready, j + 1)
                    dve.wait_ge(emb_ready, j + 1)
                    dve.tensor_tensor(X[:, 0, j, :], wave[:, j, :], EMB[j][:, :], ALU.add).then_inc(x_ready, 1)
                    dve.wait_ge(x_ready, j + 1)
                if isinstance(g, int) and g == 0:
                    dve.wait_ge(x_copied[j], 16)
                if nxt4:
                    row_stats(X[:, nxt4[0] % H, nxt4[1], :], nxt4[2], nxt4[1] % 2)
                if isinstance(g, int) and (g, j) == (-1, 0):
                    dve.wait_ge(turns_ready, 1)
                    encode_angles(2)
                    low_weights(0)
                if isinstance(g, int) and (g, j) == (-1, 1):
                    some_keys()
                if isinstance(g, int) and (g, j) == (-1, 2):
                    masks()
                if last_pair(g) and j == 1:
                    heads_norm(0)
                if last_pair(g) and j == 2:
                    encoder_output(0)
                if last_pair(g) and j == 3:
                    attention_rows(0)
                    heads_norm(1)
                    attention_square(0)
                    encoder_output(1)

            def experts_low(q):
                dve.wait_ge(ew_high, q + 1)
                dve.tensor_tensor(el[:, 4 * q:4 * q + 4, :], EW[q][:, :].rearrange("p (k d) -> p k d", k=4),
                                  eh[:, 4 * q:4 * q + 4, :].bitcast(F32), ALU.subtract).then_inc(ew_ready, 1)

            def stats_of(b, what, x):
                i = NORMS.index((b, what))
                row_stats(x, NU + i, i % 2)

            def factors(b, what):
                i = NORMS.index((b, what))
                dve.wait_ge(rstd_ready, NU + i + 1)
                return mv[i % 2][:, :, 0], mv[i % 2][:, :, 1], rstd[i % 2]

            def normalised(out_, x, mean, factor, c):
                return dve.tensor_scalar(out_, x, mean[:, c:c + 1], factor[:, c:c + 1], ALU.subtract, ALU.mult)

            def shifts(b, what, mean, factor):
                i = NORMS.index((b, what))
                dve.tensor_copy(factor_of[:, i, :], factor[:, :])
                dve.scalar_tensor_tensor(out=shift_of[:, i, :], in0=mean, scalar=-1.0, in1=factor[:, :],
                                         op0=ALU.mult, op1=ALU.mult).then_inc(shift_ready, 1)

            def heads_norm(b):
                dve.wait_ge(x_updated, NU - B + b + 1)
                stats_of(b, "heads", h0[:, b, :])

            def encoder_output(b):
                h3 = h0[:, b, :].rearrange("p (c d) -> p c d", c=NC)
                dve.wait_ge(ld_tail, 48)
                mean, _, factor = factors(b, "heads")
                for c in range(NC):
                    ins = normalised(h3[:, c, :], h3[:, c, :], mean, factor, c)
                then(ins)
                then(dve.tensor_tensor(h3, h3, fin_s[:, :].unsqueeze(1).to_broadcast([P, NC, P]), ALU.mult))
                then(dve.tensor_tensor(h3, h3, fin_b[:, :].unsqueeze(1).to_broadcast([P, NC, P]), ALU.add))
                stats_of(b, "y", h0[:, b, :])

            def attention_rows(b):
                mean, _, factor = factors(b, "y")
                shifts(b, "y", mean, factor)

            def attention_square(b):
                _, variance, factor = factors(b, "y")
                then(dve.tensor_tensor(negsq[:, :], variance, factor[:, :], ALU.mult))
                then(dve.scalar_tensor_tensor(out=negsq[:, :], in0=negsq[:, :], scalar=-float(P), in1=factor[:, :],
                                              op0=ALU.mult, op1=ALU.mult))
                dve.tensor_tensor(square[:, b, :, :], ident.unsqueeze(1).to_broadcast([P, NC, P]),
                                  negsq[:, :].unsqueeze(2).to_broadcast([P, NC, P]), ALU.mult).then_inc(square_ready, 1)

            run_steps(step)(dve)

            def attended(b):
                dve.wait_ge(tail_av, NC * (b + 1))
                dve.reciprocal(rsum[:, 0:2], OB[0][:, :, P])
                then(dve.reciprocal(rsum[:, 2:4], OB[1][:, :, P]))
                for c in range(NC):
                    ins = dve.scalar_tensor_tensor(out=h1[:, b * NC + c, :], in0=OB[c // 2][:, c % 2, 0:P], scalar=rsum[:, c:c + 1],
                                                   in1=h0[:, b, c * P:(c + 1) * P], op0=ALU.mult, op1=ALU.add)
                ins.then_inc(h1_ready, 1)

            def attended_norm(b):
                dve.wait_ge(h1_ready, b + 1)
                stats_of(b, "x3", h1[:, b * NC:(b + 1) * NC, :].rearrange("p c d -> p (c d)"))

            def experts_input(b):
                js = slice(b * NC, (b + 1) * NC)
                mean, _, factor = factors(b, "x3")
                shifts(b, "x3", mean, factor)
                then(dve.tensor_tensor(x3_0[:, js], h1[:, js, 0], mean, ALU.subtract))
                dve.tensor_tensor(x3_0[:, js], x3_0[:, js], factor[:, :], ALU.mult).then_inc(x3_0_ready, 1)

            def route(b):
                js = slice(b * NC, (b + 1) * NC)
                dve.wait_ge(logit_ready, b + 1)
                then(dve.tensor_copy(logit[:, js, :], LOGIT))
                for c in range(NC):
                    ins = dve.max(top8[:, b * NC + c, :], logit[:, b * NC + c, :])
                then(ins)
                dve.tensor_tensor(lexp[:, js, :], logit[:, js, :], top8[:, js, 0:1].to_broadcast([P, NC, E]),
                                  ALU.subtract).then_inc(lshift_ready, 1)
                for c in range(NC):
                    ins = dve.max_index(idx8[:, b * NC + c, :], top8[:, b * NC + c, :], logit[:, b * NC + c, :])
                then(ins)
                dve.tensor_tensor(route1[:, js, :], K[:, C_IOTA:C_IOTA + E].unsqueeze(1).to_broadcast([P, NC, E]),
                                  idx8[:, js, 0:1].to_broadcast([P, NC, E]), ALU.is_equal).then_inc(routed, 1)

            def choose(b):
                js = slice(b * NC, (b + 1) * NC)
                dve.wait_ge(lexp_ready, b + 1)
                dve.tensor_reduce(lsum[:, js], lexp[:, js, :], AX.X, ALU.add)
                dve.wait_ge(cum_ready, b + 1)
                then(dve.scalar_tensor_tensor(out=gate[:, js, :], in0=CUM, scalar=float(CAP) + 0.5, in1=route1[:, js, :],
                                              op0=ALU.is_le, op1=ALU.mult))
                dve.tensor_reduce(group[:, js, :], gate[:, js, :].rearrange("p c (a i) -> p c a i", i=4), AX.X,
                                  ALU.add).then_inc(group_ready, 1)
                dve.tensor_reduce(member[:, js, :], gate[:, js, :].rearrange("p c (a i) -> p c i a", i=4), AX.X, ALU.add)
                then(dve.reciprocal(rprob[:, js], lsum[:, js]))
                dve.wait_ge(group_ready, b + 1)
                dve.tensor_reduce(drop[:, js], group[:, js, :], AX.X, ALU.add)
                then(dve.tensor_tensor(member[:, js, :], member[:, js, :], rprob[:, js].unsqueeze(2).to_broadcast([P, NC, 4]),
                                       ALU.mult))
                then(dve.tensor_scalar(drop[:, js], drop[:, js], -1.0, 1.0, ALU.mult, ALU.add))
                then(dve.tensor_tensor(drop[:, js], drop[:, js], rprob[:, js], ALU.mult))
                dve.wait_ge(x3_0_ready, b + 1)
                then(dve.scalar_tensor_tensor(out=x3_0[:, js], in0=x3_0[:, js], scalar=-1.0, in1=drop[:, js],
                                              op0=ALU.add, op1=ALU.mult))
                then(dve.tensor_tensor(h1[:, js, 0], h1[:, js, 0], x3_0[:, js], ALU.add))

            def grouped_low(j):
                dve.wait_ge(grouped_high, j + 1)
                dve.tensor_tensor(tl[j % 2][:, :], SA[j % 2][:, :], th[j % 2][:, :].bitcast(F32),
                                  ALU.subtract).then_inc(grouped_ready, 1)

            def add_experts(j):
                a = acc[j % 2][:, :]
                then(dve.scalar_tensor_tensor(out=a, in0=x3[:, j, :], scalar=drop[:, j:j + 1], in1=h1[:, j, :],
                                              op0=ALU.mult, op1=ALU.add))
                dve.wait_ge(expert_out, j + 1)
                if j >= 2:
                    dve.wait_ge(stored[j % 2], 16 * (j // 2))
                for i in range(4):
                    ins = dve.scalar_tensor_tensor(out=a if i < 3 else acc_out[j % 2][:, :], in0=SC[j % 2][:, i * P:(i + 1) * P],
                                                   scalar=member[:, j, i:i + 1], in1=a, op0=ALU.mult, op1=ALU.add)
                    if i < 3:
                        then(ins)
                ins.then_inc(acc_ready, 1)

            attention_rows(1)
            heads_norm(2)
            attention_square(1)
            encoder_output(2)
            heads_norm(3)
            attended(0)
            attention_rows(2)
            attention_square(2)
            attended_norm(0)
            encoder_output(3)
            experts_input(0)
            attention_rows(3)
            attention_square(3)
            experts_low(2)
            attended(1)
            attended_norm(1)
            experts_low(3)
            experts_input(1)
            route(0)
            attended(2)
            attended_norm(2)
            choose(0)
            experts_input(2)
            route(1)
            grouped_low(0)
            attended(3)
            attended_norm(3)
            for j in range(NT):
                if j:
                    grouped_low(j)
                if j == 1: choose(1)
                if j == 3: route(2)
                if j == 5: choose(2)
                if j == 7: route(3)
                if j == 9: choose(3)
                if j: add_experts(j - 1)
                if j == 1: experts_input(3)
            add_experts(NT - 1)

        @block.gpsimd
        def _(pool):
            steps = [0]

            def pool_then(ins):
                steps[0] += 1
                ins.then_inc(pool_chain, 1)
                pool.wait_ge(pool_chain, steps[0])

            def fold_matrix(gw):
                pool.tensor_copy(lncol[:, 0:1], cols[:, bass.ds(ROW_LNS + gw, 1)])
                pool.tensor_copy(lncol[:, 1:2], cols[:, bass.ds(ROW_LNB + gw, 1)]).then_inc(lncol_ready, 1)
                apart(pool, w1_ready, gw)
                apart(pool, lncol_ready, gw + 1)
                pool.tensor_scalar(fold_t[:, 1:P], K[:, C_FOLD + 1:C_FOLD + P], lncol[:, 0:1], None, ALU.mult)
                pool.tensor_copy(fold_t[:, 0:1], lncol[:, 1:2]).then_inc(fold_ready, 1)

            def normaliser(n, i, eps):
                at_least(pool, mv_ready, n + 1)
                pool.tensor_tensor(veps[i][:, :], mv[i][:, :, 1], eps[:, :], ALU.add).then_inc(veps_ready, 1)
                at_least(pool, veps_ready, n + 1)
                at_least(pool, z_ready, n - 1)
                pool.tensor_tensor(rstd[i][:, :], veps[i][:, :], half[:, :], ALU.pow).then_inc(rstd_ready, 1)

            def weight_biases(gw):
                pool.tensor_copy(bias3[:, :], cols[:, 0:3 * NG].rearrange("p (k g) -> p g k", k=3)[:, bass.ds(gw, 1), :]
                                 .rearrange("p o k -> p (o k)")).then_inc(bias3_ready, 1)
                at_least(pool, bias3_ready, gw + 1)
                at_least(pool, w1_copied, gw + 1)
                pool.tensor_tensor(w_til[:, :, 0], w_til[:, :, 0], bias3[:, :], ALU.add).then_inc(w_til_ready, 1)

            def head_sums(b):
                pool.wait_ge(x_updated, (NG - 2) * B + b + 1)
                for h in range(1, H):
                    pool.tensor_tensor(h0[:, b, :], X[:, 0, b, :] if h == 1 else h0[:, b, :], X[:, h, b, :],
                                       ALU.add).then_inc(summed, 1)
                    if h < H - 1:
                        pool.wait_ge(summed, (H - 1) * b + h)

            def step(g, j):
                nxt4 = unit(g, j, 4)
                gw = next_pair(g)
                if j == 0 and gw is not None:
                    fold_matrix(gw)
                if j == 1 and gw is not None:
                    weight_biases(gw)
                if last_pair(g):
                    head_sums(j)
                if nxt4:
                    normaliser(nxt4[2], nxt4[1] % 2, eps_in)
                if isinstance(g, int) and g == 0:
                    q = slice(4 * j, 4 * j + 4)
                    if j == 0:
                        pool.wait_ge(ld_tail, 48)
                    pool.tensor_tensor(ew[:, q, 1:P], ew[:, q, 1:P], ew[:, q, 0:1].to_broadcast([P, 4, P - 1]),
                                       ALU.subtract).then_inc(ew_sub, 1)
                    pool.wait_ge(ew_sub, j + 1)
                    pool.tensor_copy(ew[:, q, 0], cols[:, ROW_EB + 4 * j:ROW_EB + 4 * j + 4]).then_inc(ew_folded, 1)

            pool.wait_ge(setup, 1)
            pool.wait_ge(times_ready, 1)
            encode_turns(pool, pool_then, 2)
            pool.sem_inc(turns_ready, 1)
            pool.wait_ge(cols_ready, 1)
            fold_matrix(0)
            weight_biases(0)
            run_steps(step)(pool)
            for n, (b, what) in enumerate(NORMS, NU):
                pool.wait_ge(mv_ready, n + 1)
                pool.tensor_tensor(veps[n % 2][:, :], mv[n % 2][:, :, 1], (eps_sum if what == "heads" else eps_in)[:, :],
                                   ALU.add).then_inc(veps_ready, 1)
                pool.wait_ge(veps_ready, n + 1)
                pool.tensor_tensor(rstd[n % 2][:, :], veps[n % 2][:, :], half[:, :], ALU.pow).then_inc(rstd_ready, 1)


_INS = ["x", "fside_BS_event_times", "mask_BS_i1_0", "L0_tok_type_emb", "L0_tok_Wq", "L0_tok_bq", "L0_tok_Wk",
        "L0_tok_bk", "L0_tok_Wv", "L0_tok_bv", "L0_tok_Wo", "L0_tok_bo", "L0_tok_ln_scale", "L0_tok_ln_bias",
        "L0_tok_final_scale", "L0_tok_final_bias", "L0_ffn_switch_w", "L0_ffn_switch_b", "L0_ffn_expert_w",
        "L0_ffn_expert_b"]


def kernel(**inputs):
    import concourse.bacc as bacc
    from concourse.bass_utils import run_bass_kernel_spmd

    nc = bacc.Bacc("TRN2", target_bir_lowering=False, num_devices=1)
    arrays, args = {}, []
    for name in _INS:
        a = np.ascontiguousarray(inputs[name])
        arrays[f"in_{name}"] = a
        args.append(nc.dram_tensor(f"in_{name}", a.shape, mybir.dt.from_np(a.dtype), kind="ExternalInput").ap())
    const = shape_constants()
    arrays["in_const"] = const
    args.append(nc.dram_tensor("in_const", const.shape, F32, kind="ExternalInput").ap())
    args.append(nc.dram_tensor("out_h", (B, S, P), F32, kind="ExternalOutput").ap())
    tower(nc, *args)
    r = run_bass_kernel_spmd(nc, [arrays], core_ids=[0])
    return r.results[0]["out_h"]
```
